# Optimizing a Trainium2 kernel written in Bass

```python
import numpy as np
import jax
import jax.numpy as jnp

def _softmax(x, axis=-1):
    return jax.nn.softmax(x, axis=axis)
def _gelu(x):
    return jax.nn.gelu(x, approximate=True)
def _silu(x):
    return jax.nn.silu(x)
def _sigmoid(x):
    return jax.nn.sigmoid(x)
def _layernorm(x, axis=-1, eps=1e-5):
    m = jnp.mean(x, axis=axis, keepdims=True)
    v = jnp.var(x, axis=axis, keepdims=True)
    return (x - m) / jnp.sqrt(v + eps)
def _scatter_add(tgt, idx, src, axis=0):
    return tgt.at[idx].add(src)
def _segment_sum(src, seg, n):
    return jax.ops.segment_sum(src, seg, n)

kernel_name = 'mk_conv_preact_d2_conv_nhwc256_209251'

def setup_inputs(seed: int = 0):
    np.random.seed(seed)
    _w = jnp.asarray
    def _rec_inputs():
        import jax
        import jax.numpy as jnp
        _gk = jax.random.key(seed)
        x = -0.000125 + 0.9999 * jax.random.normal(jax.random.fold_in(_gk, 1), (8, 128, 128, 256), jnp.float32)
        return x
    x = _rec_inputs()
    def _L0_conv_setup():
        import jax, jax.numpy as jnp
        import numpy as np
        B, H, W, C = (8, 128, 128, 256)
        key = jax.random.key(seed)
        k1, k2 = jax.random.split(key)
        x = jax.random.normal(k1, (B, H, W, C), dtype=jnp.float32)
        gamma = jax.random.normal(k2, (1,), dtype=jnp.float32)
        return {'x': x, 'gamma': gamma}
    _L0_conv_all = _L0_conv_setup()
    _L0_conv_in = {k: v for k, v in _L0_conv_all.items() if k in ('gamma', )}
    del _L0_conv_all

    def _L1_conv_setup():
        import jax, jax.numpy as jnp
        import numpy as np
        from jax import lax
        B, H, W, C = (8, 64, 64, 256)
        MAX_SCALE = 4
        R_RED = 8
        SCALES = [2 ** i for i in range(1, MAX_SCALE + 1)]
        EPS = 1e-07
        BN_EPS = 0.001

        def _box_sum(x, k):
            c = x.shape[-1]
            ker = jnp.ones((k, k, 1, c), x.dtype)
            return lax.conv_general_dilated(x, ker, window_strides=(1, 1), padding='SAME', dimension_numbers=('NHWC', 'HWIO', 'NHWC'), feature_group_count=c)
        key = jax.random.key(seed)
        ks = jax.random.split(key, 3)
        Cr = C // R_RED
        return {'x': jax.random.normal(ks[0], (B, H, W, C), jnp.float32), 'w1': jax.random.normal(ks[1], (C, Cr), jnp.float32) * 0.05, 'b1': jnp.zeros((Cr,), jnp.float32), 'w2': jax.random.normal(ks[2], (Cr, C), jnp.float32) * 0.05, 'b2': jnp.zeros((C,), jnp.float32), 'gamma': jnp.ones((C,), jnp.float32), 'beta': jnp.zeros((C,), jnp.float32), 'moving_mean': jnp.zeros((C,), jnp.float32), 'moving_var': jnp.ones((C,), jnp.float32)}
    _L1_conv_all = _L1_conv_setup()
    _L1_conv_in = {k: v for k, v in _L1_conv_all.items() if k in ('w1', 'b1', 'w2', 'b2', 'gamma', 'beta', 'moving_mean', 'moving_var', )}
    del _L1_conv_all

    return {
        "x": x,
        "L0_conv_gamma": _L0_conv_in["gamma"],
        "L1_conv_w1": _L1_conv_in["w1"],
        "L1_conv_b1": _L1_conv_in["b1"],
        "L1_conv_w2": _L1_conv_in["w2"],
        "L1_conv_b2": _L1_conv_in["b2"],
        "L1_conv_gamma": _L1_conv_in["gamma"],
        "L1_conv_beta": _L1_conv_in["beta"],
        "L1_conv_moving_mean": _L1_conv_in["moving_mean"],
        "L1_conv_moving_var": _L1_conv_in["moving_var"],
    }

def reference(x, L0_conv_gamma, L1_conv_w1, L1_conv_b1, L1_conv_w2, L1_conv_b2, L1_conv_gamma, L1_conv_beta, L1_conv_moving_mean, L1_conv_moving_var):
    import jax
    import jax.numpy as jnp
    def _L0_conv_ref(x, gamma):
        import jax, jax.numpy as jnp
        import numpy as np
        B, H, W, C = (8, 128, 128, 256)
        b, h, w, c = x.shape
        vec_a = x.reshape(b, h * w, c)
        aTa = jnp.einsum('bpi,bpj->bij', vec_a, vec_a)
        attn = jax.nn.softmax(aTa, axis=-1)
        aaTa = jnp.einsum('bpc,bcj->bpj', vec_a, attn)
        aaTa = aaTa.reshape(b, h, w, c)
        return gamma * aaTa + x

    def _L1_conv_ref(x, w1, b1, w2, b2, gamma, beta, moving_mean, moving_var):
        import jax, jax.numpy as jnp
        import numpy as np
        from jax import lax
        B, H, W, C = (8, 64, 64, 256)
        MAX_SCALE = 4
        R_RED = 8
        SCALES = [2 ** i for i in range(1, MAX_SCALE + 1)]
        EPS = 1e-07
        BN_EPS = 0.001

        def _box_sum(x, k):
            c = x.shape[-1]
            ker = jnp.ones((k, k, 1, c), x.dtype)
            return lax.conv_general_dilated(x, ker, window_strides=(1, 1), padding='SAME', dimension_numbers=('NHWC', 'HWIO', 'NHWC'), feature_group_count=c)
        xmin = jnp.min(x, axis=(1, 2, 3), keepdims=True)
        xmax = jnp.max(x, axis=(1, 2, 3), keepdims=True)
        x = (x - xmin) / (xmax - xmin + EPS)
        measures = jnp.stack([_box_sum(x, k) for k in SCALES], axis=-1)
        log_r = jnp.log(jnp.asarray(SCALES, jnp.float32))
        log_m = jnp.log(measures + EPS)
        lr_c = log_r - log_r.mean()
        alphas = jnp.einsum('bhwcs,s->bhwc', log_m, lr_c) / jnp.sum(lr_c ** 2)
        squeeze = alphas.mean(axis=(1, 2))
        excite = jax.nn.sigmoid(jax.nn.relu(squeeze @ w1 + b1) @ w2 + b2)
        ols_est = alphas[..., None] * log_r
        a = log_m - log_m.mean(axis=-1, keepdims=True)
        b = ols_est - ols_est.mean(axis=-1, keepdims=True)
        sim = (a * b).sum(-1) / (jnp.linalg.norm(a, axis=-1) * jnp.linalg.norm(b, axis=-1) + EPS)
        alpha_norm = (alphas - moving_mean) / jnp.sqrt(moving_var + BN_EPS) * gamma + beta
        x = x * excite[:, None, None, :]
        return sim * jax.nn.sigmoid(alpha_norm) + (1.0 - sim) * x

    def _gn(v, G=32, eps=1e-5):
        B_, H_, W_, C_ = v.shape
        g = v.reshape(B_, H_, W_, G, C_ // G)
        m = jnp.mean(g, axis=(1, 2, 4), keepdims=True)
        s = jnp.var(g, axis=(1, 2, 4), keepdims=True)
        return ((g - m) / jnp.sqrt(s + eps)).reshape(v.shape)

    def _ln_c(v, eps=1e-6):
        m = jnp.mean(v, axis=-1, keepdims=True)
        s = jnp.var(v, axis=-1, keepdims=True)
        return (v - m) / jnp.sqrt(s + eps)

    def _ln_t(v, eps=1e-5):
        m = jnp.mean(v, axis=-1, keepdims=True)
        s = jnp.var(v, axis=-1, keepdims=True)
        return (v - m) / jnp.sqrt(s + eps)

    def _to_tokens(v):
        B_, H_, W_, C_ = v.shape
        return v.reshape(B_, H_ * W_, C_)
    def _from_tokens(t, like):
        return t.reshape(like.shape)

    x = x + _L0_conv_ref(_gn(x), L0_conv_gamma)
    x = x + _L1_conv_ref(_gn(x), L1_conv_w1, L1_conv_b1, L1_conv_w2, L1_conv_b2, L1_conv_gamma, L1_conv_beta, L1_conv_moving_mean, L1_conv_moving_var)
    return x


_drawn_inputs = setup_inputs


def setup_inputs(seed=0):
    import zlib

    import numpy as np

    out = dict(_drawn_inputs(seed))
    spreads = {'L1_conv_b1': (0.0, 2.0),
     'L1_conv_b2': (0.0, 2.0),
     'L1_conv_gamma': (1.0, 0.2),
     'L1_conv_beta': (0.0, 0.733),
     'L1_conv_moving_mean': (0.0, 0.729),
     'L1_conv_moving_var': (1.0, 0.6)}
    factors = {'L1_conv_w1': 200.0, 'L1_conv_w2': 200.0}
    for name, (base, spread) in spreads.items():
        noise = np.random.default_rng([zlib.crc32(name.encode()), seed]).standard_normal(out[name].shape)
        drawn = base * np.exp(spread * noise) if base else spread * noise
        out[name] = jnp.asarray(drawn.astype(out[name].dtype))
    for name, factor in factors.items():
        out[name] = (out[name] * factor).astype(out[name].dtype)
    return out
```

```python
import math
from contextlib import ExitStack, contextmanager

import concourse.bass as bass
from concourse import mybir

F32 = mybir.dt.float32
ALU = mybir.AluOpType
ACT = mybir.ActivationFunctionType
AX_X = mybir.AxisListType.X
RMAX = bass.bass_isa.ReduceOp.max

B, H, W, C = 8, 128, 128, 256
CH = C // 2
PIX = H * W
ROWS = 8
CHUNKS = H // ROWS
PAIRS = CHUNKS // 2
SUB = 4
UNIT = ROWS * W
HIDDEN = C // 8
GROUP = C // 32
SCALES = (2, 4, 8, 16)
SLOTS = len(SCALES) + 1
GN_EPS = 1e-5
BN_EPS = 1e-3
EPS = 1e-7
LN2 = math.log(2.0)
SLOPE = 10.0 * LN2
B_NORM = 1.0 / 20.0
TINY = 1e-37
HUGE = 3.0e38
EXP_MAX = 85.0

POOL_CONST = 10 + 1 + 2 * len(SCALES) + 2
POOL_PAIR, POOL_IMAGE = 14, 121
ACT_PAIR, ACT_IMAGE = 24, 196
DVE_MIN_PAIR, DVE_PAIR, DVE_IMAGE = 4, 40, 434


class Count:

    def __init__(self, eng, sem):
        self.eng, self.sem, self.base, self.k, self.total = eng, sem, 0, 0, 0

    def one(self):
        self.k += 1
        self.total += 1
        return 1

    def now(self):
        return self.base + self.k

    @contextmanager
    def loop(self, start, stop, per_turn):
        entry, before = self.base + self.k, self.total
        with self.eng.Fori(start, stop) as i:
            self.base, self.k = entry + per_turn * (i - start), 0
            yield i
            assert self.total - before == per_turn, (self.sem, self.total - before, per_turn)
        self.base, self.k = entry, per_turn * (stop - start)
        self.total = before + per_turn * (stop - start)


def some(count):
    return not (isinstance(count, int) and count <= 0)


def mk_conv_preact(nc, x, gamma, w1, b1, w2, b2, bn_gamma, bn_beta, bn_mean, bn_var, out):
    with ExitStack() as ctx:
        def sb(name, shape, dt=F32):
            return ctx.enter_context(nc.sbuf_tensor(name, shape, dt))

        def sem(name):
            return ctx.enter_context(nc.semaphore(name))

        h_dram = nc.dram_tensor("h_scratch", (B * CHUNKS, W, ROWS * C), F32, kind="Internal").ap()
        p_dram = nc.dram_tensor("p_scratch", (B * CHUNKS * 2, CH, UNIT), F32, kind="Internal").ap()
        q_dram = nc.dram_tensor("q_scratch", (B * CHUNKS * 2, CH, UNIT), F32, kind="Internal").ap()
        x_sub = x.rearrange("b (n h) w c -> (b n) w h c", h=SUB)
        out_chunk = out.rearrange("b (n h) w c -> (b n) w h c", h=ROWS)

        xa = sb("xa", [W, 2, SUB, C + 1])
        xb = sb("xb", [W, 2, SUB, C])
        xt = sb("xt", [CH, 2, 2, 2, W])
        h_out = sb("h_out", [W, 2, ROWS, C])
        h_in = sb("h_in", [W, ROWS, C])
        v = sb("v", [W, 2, 2 * ROWS, CH])
        t2 = sb("t2", [W, 2, 2 * ROWS, CH])
        t4 = sb("t4", [W, 2, 2 * ROWS, CH])
        t8 = sb("t8", [W, 2, 2 * ROWS, CH])
        logs = sb("logs", [CH, 2, 4, UNIT])
        square = sb("square", [CH, 2, UNIT])
        ut = sb("ut", [CH, 2, UNIT])
        x1t = sb("x1t", [CH, 2, UNIT])
        pd = sb("pd", [CH, 2, UNIT])
        qd = sb("qd", [CH, 2, UNIT])
        o_sb = sb("o_sb", [W, 2, ROWS, C])

        ident = sb("ident", [128, 128])
        ones = sb("ones", [128, 128])
        zeros = sb("zeros", [128, 128])
        band = sb("band", [W, 4, W])
        group = sb("group", [128, 128])
        mix = sb("mix", [CH, 2, C])
        shift = sb("shift", [128, 2, C])
        col = sb("col", [128, 64])
        w1s = sb("w1s", [CH, 2, HIDDEN])
        w2s = sb("w2s", [HIDDEN, C])
        hid = sb("hid", [HIDDEN, 4])
        prm = sb("prm", [CH, 5, 2])

        lg = logs[:, :, :, :].rearrange("p a k n -> p (a k n)")
        gram = lg[:, 0:512].rearrange("p (h c) -> p h c", h=2)
        diag = lg[:, 512:1280].rearrange("p (k c) -> p k c", k=6)
        rows = lg[:, 1280:2048].rearrange("p (k c) -> p k c", k=3)
        attn = lg[:, 2048:2560].rearrange("p (h c) -> p h c", h=2)
        step = lg[:, 2560:3072].rearrange("p (h c) -> p h c", h=2)
        full = lg[:, 3072:3584].rearrange("p (h c) -> p h c", h=2)
        gramc = lg[:, 3584:4096].rearrange("p (h c) -> p h c", h=2)
        prod = lg[:, 4096:4608].rearrange("p (h c) -> p h c", h=2)
        mrep = lg[:, 4608:4864].rearrange("p (h c) -> p h c", h=2)
        junk = lg[:, 4864:4992]

        def cols(at, n=2):
            return col[:, at:at + n]
        (SUM, SQ, MEAN, VAR, RS, TMP, NMEAN, WGT, NMAX, ESUM, GR, DSM, MU, M2, M1, V1, R1, RI, NSP) = range(0, 38, 2)
        GAM, HMAX, HMIN, MX, MNP, RNG, INV, NEGMIN = 38, 39, 40, 41, 45, 46, 47, 48
        XS, XK, GS, GB, NE, ACC, TACC = 49, 51, 53, 55, 57, 59, 61
        MN1 = 62
        cst = sb("cst", [128, 4])
        C_EPS, C_TINY, C_ONE, C_GN = range(4)
        gate = sb("gate", [128, 8])
        mx = sb("mx", [128, 4])
        rr = sb("rr", [128, 4])

        def bank(name, n=1):
            return ctx.enter_context(nc.psum_tensor(name, [128, n * 512], F32))
        g_ps = bank("g_ps")
        xt_ps = bank("xt_ps")
        h_ps = bank("h_ps")
        o_ps = bank("o_ps")
        slot = [bank("slot0", 2), bank("slot1", 2)]

        const_loaded = sem("const_loaded")
        pool_const = sem("pool_const")
        const_ready = sem("const_ready")
        xa_loaded = [sem("xa_loaded0"), sem("xa_loaded1")]
        xb_loaded = [sem("xb_loaded0"), sem("xb_loaded1")]
        xa_used = sem("xa_used")
        xt_filled = sem("xt_filled")
        xt_copied = sem("xt_copied")
        h_filled = sem("h_filled")
        h_copied = sem("h_copied")
        h_stored = [sem("h_stored0"), sem("h_stored1")]
        h_loaded = sem("h_loaded")
        v_done = sem("v_done")
        t_ready = sem("t_ready")
        slot_filled = sem("slot_filled")
        slot_read = sem("slot_read")
        slopes = sem("slopes")
        squares = sem("squares")
        low_ready = sem("low_ready")
        z_ready = sem("z_ready")
        inv_ready = sem("inv_ready")
        x1_ready = sem("x1_ready")
        tail_done = sem("tail_done")
        pq_stored = [sem("pq_stored0"), sem("pq_stored1")]
        pq_loaded = [sem("pq_loaded0"), sem("pq_loaded1")]
        sum_ready = sem("sum_ready")
        o_filled = sem("o_filled")
        o_copied = sem("o_copied")
        o_stored = [sem("o_stored0"), sem("o_stored1")]
        dve_done = sem("dve_done")
        act_done = sem("act_done")
        pool_done = sem("pool_done")
        pool_apart, dve_apart, sp_apart = sem("pool_apart"), sem("dve_apart"), sem("sp_apart")
        gram_copied = sem("gram_copied"); gram_turned = sem("gram_turned"); gram_whole = sem("gram_whole")
        group_sums = sem("group_sums"); var_ready = sem("var_ready"); rs_guess = sem("rs_guess")
        diag_ready = sem("diag_ready"); rows_ready = sem("rows_ready"); logits_ready = sem("logits_ready")
        exp_ready = sem("exp_ready"); step_ready = sem("step_ready"); mean_ready = sem("mean_ready")
        gramc_ready = sem("gramc_ready"); cov_ready = sem("cov_ready"); prod_ready = sem("prod_ready")
        var1_sums = sem("var1_sums"); mom_ready = sem("mom_ready"); mom_group = sem("mom_group")
        var1_ready = sem("var1_ready"); rs1_guess = sem("rs1_guess"); diag1_ready = sem("diag1_ready")
        rows1_ready = sem("rows1_ready"); mix_ready = sem("mix_ready")
        range_in = sem("range_in"); range_out = sem("range_out"); range_ready = sem("range_ready")
        sums_ready = sem("sums_ready"); hidden_ps = sem("hidden_ps"); hidden_ready = sem("hidden_ready")
        gate_ps = sem("gate_ps"); gate_arg = sem("gate_arg"); gate_exp = sem("gate_exp"); gate_ready = sem("gate_ready")
        bn_logs = sem("bn_logs")

        block = ctx.enter_context(nc.Block())

        def images(loop, turn):
            for s in range(3):
                turn(s, True, s >= 1, s >= 2, False)
            with loop(3, B) as s:
                turn(s, True, True, True, True)
            for s in range(B, B + 3):
                turn(s, False, s <= B, s <= B + 1, True)

        @block.sync
        def _(sp):
            def apart():
                sp.sem_inc(sp_apart, 1)

            for dst, src in ((w1s[:, :, :], w1.rearrange("(h c) r -> c h r", h=2)), (w2s[:, :], w2),
                             (hid[:, 0:1], b1.rearrange("(r o) -> r o", o=1)),
                             (col[:, GAM:GAM + 1], gamma.rearrange("(a o) -> a o", o=1).to_broadcast([128, 1]))):
                sp.dma_start(dst, src).then_inc(const_loaded, 16)
            with nc.allow_non_contiguous_dma(reason="five short parameter columns"):
                for k, src in enumerate((bn_gamma, bn_beta, bn_mean, bn_var, b2)):
                    sp.dma_start(prm[:, k, :], src.rearrange("(h c) -> c h", h=2)).then_inc(const_loaded, 16)

            def chunk(s, i, k, A, Bs, Cs, Ds, first, last):
                c = 2 * i + k
                n = 16 * s + c
                nb, nC, nd = n - 16, n - 32, n - 48
                prev = not (first and k == 0)
                for hf in range(2):
                    if Cs and hf == 0 and not (last and k == 1):
                        sp.wait_ge(v_done, 2 * (nC + 1))
                        apart()
                        sp.dma_start(h_in[:, :, :].rearrange("p r c -> p (r c)"),
                                     h_dram[nC + 1]).then_inc(h_loaded, 16)
                    if A:
                        sp.wait_ge(xa_used, 2 * n + hf + 1)
                        apart()
                        sp.dma_start(xa[:, hf, :, 0:C], x_sub[2 * n + hf]).then_inc(xa_loaded[hf], 16)
                    if Bs:
                        if some(4 * nb + 2 * hf):
                            sp.wait_ge(xt_filled, 4 * nb + 2 * hf)
                        apart()
                        sp.dma_start(xb[:, hf, :, :], x_sub[2 * nb + hf]).then_inc(xb_loaded[hf], 16)
                    if Ds:
                        sp.wait_ge(o_filled, 2 * (2 * nd + hf))
                        apart()
                        sp.dma_start(pd[:, hf, :], p_dram[2 * nd + hf]).then_inc(pq_loaded[hf], 16)
                        sp.dma_start(qd[:, hf, :], q_dram[2 * nd + hf]).then_inc(pq_loaded[hf], 16)
                    if Cs and hf == 0 and not first:
                        store_pq(2 * nC - 3, 1)
                    if Cs and hf == 1 and prev:
                        store_pq(2 * nC - 2, 0)
                    if Bs and hf == 1 and prev:
                        sp.wait_ge(h_copied, 4 * nb + 1)
                        apart()
                        sp.dma_start(h_dram[nb - 1], h_out[:, 1 - k, :, :].rearrange("p r c -> p (r c)")
                                     ).then_inc(h_stored[1 - k], 16)
                    if Ds and hf == 1 and prev:
                        sp.wait_ge(o_copied, 4 * nd + 1)
                        apart()
                        sp.dma_start(out_chunk[nd - 1], o_sb[:, 1 - k, :, :]).then_inc(o_stored[1 - k], 16)

            def store_pq(unit, hf):
                sp.wait_ge(tail_done, unit + 3)
                apart()
                sp.dma_start(p_dram[unit], x1t[:, hf, :]).then_inc(pq_stored[hf], 16)
                sp.dma_start(q_dram[unit], ut[:, hf, :]).then_inc(pq_stored[hf], 16)

            def turn(s, A, Bs, Cs, Ds):
                if Ds:
                    for p in pq_stored:
                        sp.wait_ge(p, 32 * CHUNKS * (s - 2))
                        apart()
                if Cs:
                    for p in h_stored:
                        sp.wait_ge(p, 16 * PAIRS * (s - 1))
                        apart()
                    if some(32 * (s - 2)):
                        sp.wait_ge(v_done, 32 * (s - 2))
                    apart()
                    sp.dma_start(h_in[:, :, :].rearrange("p r c -> p (r c)"),
                                 h_dram[16 * (s - 2)]).then_inc(h_loaded, 16)

                def pair(i, first, last):
                    for k in range(2):
                        chunk(s, i, k, A, Bs, Cs, Ds, first, last)
                pair(0, True, False)
                with sp.Fori(1, PAIRS - 1) as i:
                    pair(i, False, False)
                pair(PAIRS - 1, False, True)
                n = 16 * (s + 1)
                if Cs:
                    store_pq(2 * (n - 32) - 3, 1)
                if Bs:
                    sp.wait_ge(h_copied, 4 * (n - 16) + 1)
                    apart()
                    sp.dma_start(h_dram[n - 17], h_out[:, 1, :, :].rearrange("p r c -> p (r c)")
                                 ).then_inc(h_stored[1], 16)
                if Ds:
                    sp.wait_ge(o_copied, 4 * (n - 48) + 1)
                    apart()
                    sp.dma_start(out_chunk[n - 49], o_sb[:, 1, :, :]).then_inc(o_stored[1], 16)
                if Cs:
                    for left in (2, 1):
                        store_pq(2 * (n - 32) - left, left % 2)

            images(sp.Fori, turn)
            for p in o_stored:
                sp.wait_ge(p, 16 * PAIRS * B)
                apart()

        @block.gpsimd
        def _(pool):
            g = nc.gpsimd
            g.memset(ident[:, :], 0.0).then_inc(pool_const, 1)
            g.memset(ones[:, :], 1.0).then_inc(pool_const, 1)
            g.memset(band[:, :, :], 1.0).then_inc(pool_const, 1)
            g.memset(group[:, :], 1.0 / GROUP).then_inc(pool_const, 1)
            g.memset(xa[:, :, :, C:C + 1], 1.0).then_inc(pool_const, 1)
            for j, value in enumerate((EPS, TINY, 1.0, GN_EPS)):
                g.memset(cst[:, j:j + 1], value).then_inc(pool_const, 1)
            g.memset(mx[:, :], -HUGE).then_inc(pool_const, 1)
            pool.wait_ge(pool_const, 10)
            made = 10
            g.affine_select(out=ident[:, :], in_=ident[:, :], compare_op=ALU.not_equal, fill=1.0, base=0,
                            pattern=[[-1, 128]], channel_multiplier=1).then_inc(pool_const, 1)
            for k, size in enumerate(SCALES):
                lo = (size - 1) // 2
                hi = size - 1 - lo
                pool.wait_ge(pool_const, made + 1)
                g.affine_select(out=band[:, k, :], in_=band[:, k, :], compare_op=ALU.is_ge, fill=0.0, base=lo,
                                pattern=[[-1, W]], channel_multiplier=1).then_inc(pool_const, 1)
                pool.wait_ge(pool_const, made + 2)
                g.affine_select(out=band[:, k, :], in_=band[:, k, :], compare_op=ALU.is_ge, fill=0.0, base=hi,
                                pattern=[[1, W]], channel_multiplier=-1).then_inc(pool_const, 1)
                made += 2
            gv = group[:, :].rearrange("p (g c) -> p g c", c=GROUP)
            pool.wait_ge(pool_const, made + 1)
            g.affine_select(out=gv, in_=gv, compare_op=ALU.is_ge, fill=0.0, base=0,
                            pattern=[[-GROUP, 128 // GROUP], [0, GROUP]], channel_multiplier=1).then_inc(pool_const, 1)
            pool.wait_ge(pool_const, made + 2)
            g.affine_select(out=gv, in_=gv, compare_op=ALU.is_ge, fill=0.0, base=GROUP - 1,
                            pattern=[[GROUP, 128 // GROUP], [0, GROUP]], channel_multiplier=-1).then_inc(pool_const, 1)
            assert made + 3 == POOL_CONST
            own = Count(pool, pool_done)

            def apart():
                pool.sem_inc(pool_apart, 1)

            def add_rows(dst, src, hf, k, gap, final):
                a = k * ROWS
                if k == 1:
                    parts = [(a, a - gap, ROWS)]
                else:
                    parts = [(a, 2 * ROWS - gap, gap), (a + gap, a, ROWS - gap)]
                for d, e, n in parts:
                    ins = g.tensor_tensor(dst[:, hf, d:d + n, :], src[:, hf, d:d + n, :], src[:, hf, e:e + n, :], ALU.add)
                    if final and (d, e, n) == parts[-1]:
                        ins.then_inc(t_ready, 1)
                    else:
                        ins.then_inc(pool_done, own.one())

            def row_sums(s, c, k, hf, load):
                a = k * ROWS
                if load is None:
                    apart()
                    g.memset(v[:, hf, a:a + ROWS, :], 0.0).then_inc(pool_done, own.one())
                    pool.wait_ge(pool_done, own.now())
                else:
                    pool.wait_ge(h_loaded, 16 * (load + 1))
                    apart()
                    g.tensor_scalar(v[:, hf, a:a + ROWS, :], h_in[:, :, hf * CH:(hf + 1) * CH],
                                    col[:, NEGMIN:NEGMIN + 1], col[:, INV:INV + 1], ALU.add, ALU.mult).then_inc(v_done, 1)
                    pool.wait_ge(v_done, 2 * load + hf + 1)
                add_rows(t2, v, hf, k, 1, False)
                pool.wait_ge(pool_done, own.now())
                add_rows(t4, t2, hf, k, 2, False)
                pool.wait_ge(pool_done, own.now())
                add_rows(t8, t4, hf, k, 4, True)

            def low_difference(unit, hf):
                pool.wait_ge(slot_read, 2 + SLOTS * unit + 2)
                g.tensor_tensor(square[:, hf, :], logs[:, hf, 0, :], logs[:, hf, 1, :], ALU.subtract).then_inc(low_ready, 1)

            def make_x1(unit, hf):
                pool.wait_ge(slot_read, 2 + SLOTS * unit + SLOTS)
                apart()
                g.tensor_scalar(x1t[:, hf, :], ut[:, hf, :], col[:, XS + hf:XS + hf + 1], col[:, XK + hf:XK + hf + 1],
                                ALU.mult, ALU.add).then_inc(x1_ready, 1)

            def turn(s, A, Bs, Cs, Ds):
                if Cs:
                    image = s - 2
                    pool.wait_ge(range_ready, s - 1)
                    if not (isinstance(s, int) and s == 2):
                        pool.wait_ge(slot_filled, SLOTS * 32 * image)
                    apart()
                    g.memset(v[:, :, ROWS - 1:ROWS, :], 0.0).then_inc(pool_done, own.one())
                    g.memset(t2[:, :, ROWS - 2:ROWS, :], 0.0).then_inc(pool_done, own.one())
                    g.memset(t4[:, :, ROWS - 4:ROWS, :], 0.0).then_inc(pool_done, own.one())
                    pool.wait_ge(pool_done, own.now())
                    for hf in range(2):
                        row_sums(s, None, 1, hf, 16 * image)

                    def pair(i, first, last):
                        for k in range(2):
                            n = 16 * image + 2 * i + k
                            for hf in range(2):
                                unit = 2 * n + hf
                                if not (first and k == 0):
                                    pool.wait_ge(slot_filled, SLOTS * (unit - 1))
                                row_sums(s, n, k, hf, None if last and k == 1 else n + 1)
                                if not (first and k == 0 and hf == 0):
                                    make_x1(unit - 1, 1 - hf)
                                low_difference(unit, hf)
                    pair(0, True, False)
                    with own.loop(1, PAIRS - 1, POOL_PAIR) as i:
                        pair(i, False, False)
                    pair(PAIRS - 1, False, True)
                    make_x1(32 * (image + 1) - 1, 1)
                if Bs:
                    pool.wait_ge(range_in, s)
                    apart()
                    g.partition_all_reduce(rr[:, 2:4], rr[:, 0:2], 128, RMAX).then_inc(range_out, 1)

            images(lambda lo, hi: own.loop(lo, hi, POOL_IMAGE), turn)

        @block.tensor
        def _(pe):
            t = nc.tensor
            pe.sem_inc(xa_used, 2)
            pe.sem_inc(xt_filled, 2)
            pe.sem_inc(h_filled, 2)
            pe.sem_inc(o_filled, 2)
            pe.wait_ge(const_ready, 1)

            def gram_rows(n, hf, half):
                if half == 0:
                    pe.wait_ge(xa_loaded[hf], 16 * (n + 1))
                for r in (2 * half, 2 * half + 1):
                    xr = xa[:, hf, r, :]
                    t.matmul(g_ps[:, 0:C + 1], xr[:, 0:CH], xr[:, :], start=False, stop=False, skip_group_check=True)
                    ins = t.matmul(g_ps[:, C + 1:C + 2 + CH], xr[:, CH:C], xr[:, CH:C + 1], start=False, stop=False,
                                   skip_group_check=True)
                if half == 1:
                    ins.then_inc(xa_used, 1)

            def turn_x(n, q):
                m = 4 * n + q
                if q % 2 == 0:
                    pe.wait_ge(xb_loaded[q // 2], 16 * (n + 1))
                pe.wait_ge(xt_copied, m + 1)
                for jh in range(2):
                    for r in range(2):
                        ins = t.transpose(xt_ps[:, (2 * jh + r) * W:(2 * jh + r + 1) * W],
                                          xb[:, q // 2, 2 * (q % 2) + r, jh * CH:(jh + 1) * CH], ident[:, :])
                ins.then_inc(xt_filled, 1)

            def mix_x(n, q):
                m = 4 * n + q
                pe.wait_ge(xt_copied, m + 2)
                pe.wait_ge(h_copied, m + 1)
                for r in range(2):
                    for jh in range(2):
                        ins = t.matmul(h_ps[:, r * C:(r + 1) * C], xt[:, q % 2, jh, r, :], mix[:, jh, :],
                                       start=(jh == 0), stop=(jh == 1))
                ins.then_inc(h_filled, 1)

            def box(unit, k, hf, which):
                s = SLOTS * unit + which
                pe.wait_ge(slot_read, s + 1)
                dst = slot[(hf + which) % 2]
                new, old = k * ROWS, (1 - k) * ROWS
                for j in range(ROWS):
                    o = dst[:, j * W:(j + 1) * W]
                    if which == 4:
                        ins = t.transpose(o, v[:, hf, old + j, :], ident[:, :])
                        continue
                    src, lag = ((t2, 1), (t4, 2), (t8, 4), (t8, 0))[which]
                    at = old + lag + j if lag + j < ROWS else new + lag + j - ROWS
                    ins = t.matmul(o, src[:, hf, at, :], band[:, which, :], start=True, stop=(which < 3))
                    if which == 3:
                        ins = t.matmul(o, t8[:, hf, new + j, :], band[:, which, :], start=False, stop=True)
                ins.then_inc(slot_filled, 1)

            def turn_back(unit, hf, d):
                if d == 0:
                    pe.wait_ge(sum_ready, unit + 1)
                pe.wait_ge(o_copied, 2 * unit + d + 1)
                for r in range(4):
                    ins = t.transpose(o_ps[:, r * CH:(r + 1) * CH], pd[:, hf, (4 * d + r) * W:(4 * d + r + 1) * W],
                                      ident[:, :])
                ins.then_inc(o_filled, 1)

            def half_chunk(n, i, k, hf, A, Bs, Cs, Ds):
                nb, nC, nd = n - 16, n - 32, n - 48
                u = 2 * nC + hf
                if Cs:
                    pe.wait_ge(t_ready, u + 3 + 2 * image_of[0])
                    box(u, k, hf, 0)
                if Bs:
                    turn_x(nb, 2 * hf)
                if Cs:
                    box(u, k, hf, 1)
                if A:
                    gram_rows(n, hf, 0)
                if Cs:
                    box(u, k, hf, 2)
                if Bs:
                    mix_x(nb, 2 * hf)
                    turn_x(nb, 2 * hf + 1)
                if Ds:
                    turn_back(2 * nd + hf, hf, 0)
                if Cs:
                    box(u, k, hf, 3)
                if A:
                    gram_rows(n, hf, 1)
                if Bs:
                    mix_x(nb, 2 * hf + 1)
                if Cs:
                    box(u, k, hf, 4)
                if Ds:
                    turn_back(2 * nd + hf, hf, 1)

            image_of = [None]

            def turn(s, A, Bs, Cs, Ds):
                image_of[0] = s - 2
                if Bs:
                    pe.wait_ge(mix_ready, s)
                if A:
                    if not (isinstance(s, int) and s == 0):
                        pe.wait_ge(gram_copied, s)
                    t.matmul(g_ps[:, :], zeros[:, :], band[:, :, :].rearrange("p k w -> p (k w)"), start=True, stop=False, skip_group_check=True)
                def pair(i):
                    for k in range(2):
                        for hf in range(2):
                            half_chunk(16 * s + 2 * i + k, i, k, hf, A, Bs, Cs, Ds)
                with pe.Fori(0, PAIRS) as i:
                    pair(i)
                if Ds:
                    pe.wait_ge(o_copied, 64 * (s - 2) + 1)
                if Cs:
                    excite(s - 2)
                if A:
                    stats(s)

            def excite(b):
                pe.wait_ge(sums_ready, b + 1)
                for h in range(2):
                    ins = t.matmul(o_ps[0:HIDDEN, 0:1], w1s[:, h, :], gate[:, h:h + 1], start=(h == 0), stop=(h == 1))
                ins.then_inc(hidden_ps, 1)
                pe.wait_ge(hidden_ready, b + 1)
                for h in range(2):
                    ins = t.matmul(o_ps[:, 8 + h:9 + h], w2s[:, h * CH:(h + 1) * CH], hid[:, 2:3], start=True, stop=True)
                ins.then_inc(gate_ps, 1)

            def stats(b):
                pe.wait_ge(gram_copied, b + 1)
                t.transpose(xt_ps[:, 0:CH], gram[:, 0, CH:C], ident[:, :]).then_inc(gram_turned, 1)
                pe.wait_ge(gram_whole, b + 1)
                t.matmul(h_ps[:, 0:4], group[:, :], cols(SUM, 4), start=True, stop=True).then_inc(group_sums, 1)
                pe.wait_ge(diag_ready, b + 1)
                for k in range(4):
                    t.matmul(xt_ps[:, k * 128:(k + 1) * 128], ones[:, :], diag[:, k, :], start=True, stop=True)
                for k in range(2):
                    ins = t.matmul(h_ps[:, 256 + k * 128:256 + (k + 1) * 128], ones[:, :], diag[:, 4 + k, :],
                                   start=True, stop=True)
                ins.then_inc(rows_ready, 1)
                pe.wait_ge(step_ready, b + 1)
                for ch in range(2):
                    for jh in range(2):
                        t.matmul(xt_ps[:, ch:ch + 1], step[:, jh, ch * CH:(ch + 1) * CH], cols(DSM)[:, jh:jh + 1],
                                 start=(jh == 0), stop=(jh == 1))
                for jh in range(2):
                    ins = t.matmul(h_ps[:, 0:C], mrep[:, jh, :], step[:, jh, :], start=(jh == 0), stop=(jh == 1))
                ins.then_inc(mean_ready, 1)
                pe.wait_ge(gramc_ready, b + 1)
                for ih in range(2):
                    for jh in range(2):
                        ins = t.matmul(o_ps[:, ih * C:(ih + 1) * C], gramc[:, jh, ih * CH:(ih + 1) * CH], full[:, jh, :],
                                       start=(jh == 0), stop=(jh == 1))
                ins.then_inc(cov_ready, 1)
                pe.wait_ge(prod_ready, b + 1)
                for ch in range(2):
                    for ih in range(2):
                        ins = t.matmul(g_ps[:, 8 + ch:9 + ch], prod[:, ih, ch * CH:(ch + 1) * CH], ones[:, 0:1],
                                       start=(ih == 0), stop=(ih == 1))
                ins.then_inc(var1_sums, 1)
                pe.wait_ge(mom_ready, b + 1)
                t.matmul(g_ps[:, 16:20], group[:, :], cols(MU, 4), start=True, stop=True).then_inc(mom_group, 1)
                pe.wait_ge(diag1_ready, b + 1)
                for k in range(4):
                    ins = t.matmul(o_ps[:, k * 128:(k + 1) * 128], ones[:, :], diag[:, k, :], start=True, stop=True)
                ins.then_inc(rows1_ready, 1)

            images(pe.Fori, turn)

        @block.scalar
        def _(act):
            a = nc.scalar
            a.preload_act_table_set("natural_log_exp_and_others")
            act.sem_inc(slot_read, 2)
            act.sem_inc(xt_copied, 1)
            act.sem_inc(o_copied, 1)
            act.wait_ge(const_ready, 1)
            own = Count(act, act_done)

            def const(j):
                return cst[:, j:j + 1]

            a.activation(cols(TMP), prm[:, 3, :], ACT.Ln, bias=col[:, 63:64]).then_inc(bn_logs, 1)
            act.wait_ge(bn_logs, 1)
            a.activation(cols(GS), cols(TMP), ACT.Exp, scale=-0.5).then_inc(bn_logs, 1)

            def copy_xt(n, q):
                m = 4 * n + q
                act.wait_ge(xt_filled, m + 3)
                act.wait_ge(h_filled, m + 1)
                a.activation(xt[:, q % 2, :, :, :].rearrange("p j r w -> p (j r w)"), xt_ps[:, :], ACT.Copy
                             ).then_inc(xt_copied, 1)

            def log(unit, n, hf, which):
                s = SLOTS * unit + which
                src = slot[(hf + which) % 2]
                act.wait_ge(slot_filled, s + 1)
                if which == 0 and some(unit - 1):
                    act.wait_ge(z_ready, unit - 1)
                if which == 1:
                    act.wait_ge(tail_done, unit + 1)
                if which == 4:
                    if some(32 * n):
                        act.wait_ge(pq_stored[hf], 32 * n)
                    a.activation(ut[:, hf, :], src[:, :], ACT.Copy).then_inc(slot_read, 1)
                else:
                    a.activation(logs[:, hf, which, :], src[:, :], ACT.Ln, bias=const(C_EPS)).then_inc(slot_read, 1)

            def square_logs(unit, hf):
                act.wait_ge(slopes, unit + 1)
                for k, scale in ((3, math.sqrt(0.5)), (2, math.sqrt(0.5)), (0, 0.5)):
                    lk = logs[:, hf, k, :]
                    a.activation(lk, lk, ACT.Square, scale=scale).then_inc(squares, 1)
                a.activation(square[:, hf, :], logs[:, hf, 1, :], ACT.Square).then_inc(squares, 1)

            def sigmoid(unit, hf, steps):
                lk = logs[:, hf, 1, :]
                if 0 in steps:
                    a.activation(lk, lk, ACT.Exp, bias=col[:, GB + hf:GB + hf + 1], scale=col[:, GS + hf:GS + hf + 1]
                                 ).then_inc(act_done, own.one())
                if 1 in steps:
                    act.wait_ge(act_done, own.now())
                    a.activation(lk, lk, ACT.Ln, bias=const(C_ONE)).then_inc(act_done, own.one())
                if 2 in steps:
                    act.wait_ge(act_done, own.now())
                    a.activation(lk, lk, ACT.Exp, scale=-1.0).then_inc(act_done, own.one())

            def invert(unit, hf, steps):
                lk = logs[:, hf, 3, :]
                if 0 in steps:
                    act.wait_ge(z_ready, unit + 1)
                    a.activation(lk, lk, ACT.Ln, bias=const(C_TINY), scale=B_NORM).then_inc(act_done, own.one())
                if 1 in steps:
                    act.wait_ge(act_done, own.now())
                    a.activation(lk, lk, ACT.Exp, scale=0.5).then_inc(act_done, own.one())
                if 2 in steps:
                    act.wait_ge(act_done, own.now())
                    a.activation(lk, lk, ACT.Ln, bias=const(C_EPS)).then_inc(act_done, own.one())
                if 3 in steps:
                    act.wait_ge(act_done, own.now())
                    a.activation(lk, lk, ACT.Exp, scale=-1.0).then_inc(inv_ready, 1)

            def copy_out(n, unit, hf, d, k, stored):
                act.wait_ge(o_filled, 2 * unit + d + 3)
                if hf == 0 and d == 0 and some(stored):
                    act.wait_ge(o_stored[k], stored)
                a.activation(o_sb[:, k, 4 * d:4 * d + 4, hf * CH:(hf + 1) * CH],
                             o_ps[:, :].rearrange("p (r c) -> p r c", c=CH), ACT.Copy).then_inc(o_copied, 1)

            def half_chunk(s, i, k, hf, A, Bs, Cs, Ds, first):
                n = 16 * s + 2 * i + k
                nb, nC, nd = n - 16, n - 32, n - 48
                u, ud = 2 * nC + hf, 2 * nd + hf
                tail = Cs and not first
                if Cs:
                    log(u, nC, hf, 0)
                if tail:
                    square_logs(u - 1, 1 - hf)
                if Bs:
                    copy_xt(nb, 2 * hf)
                if Cs:
                    log(u, nC, hf, 1)
                if tail:
                    sigmoid(u - 1, 1 - hf, (0, 1))
                if Ds:
                    copy_out(nd, ud, hf, 0, k, 16 * (8 * (s - 3) + i))
                if Cs:
                    log(u, nC, hf, 2)
                if tail:
                    invert(u - 1, 1 - hf, (0, 1))
                if Bs:
                    copy_xt(nb, 2 * hf + 1)
                if Cs:
                    log(u, nC, hf, 3)
                if tail:
                    sigmoid(u - 1, 1 - hf, (2,))
                    invert(u - 1, 1 - hf, (2, 3))
                if Cs:
                    log(u, nC, hf, 4)
                if Ds:
                    copy_out(nd, ud, hf, 1, k, None)

            def turn(s, A, Bs, Cs, Ds):
                if Cs:
                    act.wait_ge(mix_ready, s if not isinstance(s, int) else min(s, B))

                def pair(i, first):
                    for k in range(2):
                        for hf in range(2):
                            half_chunk(s, i, k, hf, A, Bs, Cs, Ds, first and k == 0 and hf == 0)
                pair(0, True)
                with own.loop(1, PAIRS, ACT_PAIR if Cs else 0) as i:
                    pair(i, False)
                if Cs:
                    u = 32 * (s - 1)
                    square_logs(u - 1, 1)
                    sigmoid(u - 1, 1, (0, 1, 2))
                    invert(u - 1, 1, (0, 1, 2, 3))
                    b = s - 2
                    act.wait_ge(gate_arg, b + 1)
                    a.activation(gate[:, 4:6], gate[:, 2:4], ACT.Exp).then_inc(gate_exp, 1)
                if A:
                    b = s
                    for ready, var, rs, guess in ((var_ready, VAR, RS, rs_guess), (None,) * 4, (var1_ready, V1, R1, rs1_guess)):
                        if ready is None:
                            act.wait_ge(logits_ready, b + 1)
                            for h in range(2):
                                a.activation(attn[:, h, :], attn[:, h, :], ACT.Exp,
                                             bias=cols(NMAX)[:, h:h + 1], accum_out=cols(ESUM)[:, h:h + 1]).then_inc(act_done, own.one())
                            act.wait_ge(act_done, own.now())
                            a.activation(cols(TMP), cols(ESUM), ACT.Copy).then_inc(exp_ready, 1)
                            continue
                        act.wait_ge(ready, b + 1)
                        a.activation(cols(rs), cols(var), ACT.Ln, bias=const(C_GN)).then_inc(act_done, own.one())
                        act.wait_ge(act_done, own.now())
                        a.activation(cols(rs), cols(rs), ACT.Exp, scale=-0.5).then_inc(guess, 1)

            images(lambda lo, hi: own.loop(lo, hi, ACT_IMAGE), turn)

        @block.vector
        def _(dve):
            d = nc.vector
            dve.sem_inc(tail_done, 2)
            dve.sem_inc(h_copied, 1)
            own = Count(dve, dve_done)

            def apart():
                dve.sem_inc(dve_apart, 1)

            dve.wait_ge(pool_const, POOL_CONST)
            dve.wait_ge(const_loaded, 16 * 9)
            d.memset(zeros[:, :], 0.0).then_inc(dve_done, own.one())
            d.memset(col[:, 63:64], BN_EPS).then_inc(dve_done, own.one())
            d.tensor_scalar(gate[:, 6:8], prm[:, 4, :], -1.0, None, ALU.mult).then_inc(dve_done, own.one())
            dve.wait_ge(dve_done, own.now())
            d.tensor_copy(hid[:, 1:2], hid[:, 0:1]).then_inc(const_ready, 1)
            dve.wait_ge(bn_logs, 2)
            newton_v, y = cols(V1), cols(GS)
            d.tensor_scalar(newton_v, prm[:, 3, :], BN_EPS, None, ALU.add).then_inc(dve_done, own.one())

            def newton(var, y):
                dve.wait_ge(dve_done, own.now())
                d.tensor_tensor(cols(TMP), var, y, ALU.mult).then_inc(dve_done, own.one())
                dve.wait_ge(dve_done, own.now())
                d.tensor_tensor(cols(TMP), cols(TMP), y, ALU.mult).then_inc(dve_done, own.one())
                dve.wait_ge(dve_done, own.now())
                d.tensor_scalar(cols(TMP), cols(TMP), -0.5, 1.5, ALU.mult, ALU.add).then_inc(dve_done, own.one())
                dve.wait_ge(dve_done, own.now())
                d.tensor_tensor(y, y, cols(TMP), ALU.mult).then_inc(dve_done, own.one())
                dve.wait_ge(dve_done, own.now())
            newton(newton_v, y)
            d.tensor_tensor(y, y, prm[:, 0, :], ALU.mult).then_inc(dve_done, own.one())
            dve.wait_ge(dve_done, own.now())
            d.tensor_tensor(cols(GB), y, prm[:, 2, :], ALU.mult).then_inc(dve_done, own.one())
            dve.wait_ge(dve_done, own.now())
            d.tensor_tensor(cols(GB), cols(GB), prm[:, 1, :], ALU.subtract).then_inc(dve_done, own.one())
            d.tensor_scalar(y, y, -1.0 / SLOPE, None, ALU.mult).then_inc(dve_done, own.one())
            dve.wait_ge(dve_done, own.now())

            def copy_h(n, k, q, first, stored):
                m = 4 * n + q
                dve.wait_ge(h_filled, m + 3)
                if q == 0 and some(stored):
                    dve.wait_ge(h_stored[k], stored)
                apart()
                d.tensor_tensor_reduce(h_out[:, k, 2 * q:2 * q + 2, :].rearrange("p r c -> p (r c)"), h_ps[:, :],
                                       shift[:, :, :].rearrange("p r c -> p (r c)"), 1.0,
                                       mx[:, (q - 1) % 4:(q - 1) % 4 + 1], ALU.add, ALU.max,
                                       mx[:, q:q + 1]).then_inc(h_copied, 1)
                dve.wait_ge(h_copied, m + 2)

            def min_h(k):
                d.tensor_reduce(col[:, MN1:MN1 + 1], h_out[:, k, :, :].rearrange("p r c -> p (r c)"), AX_X, ALU.min).then_inc(dve_done, own.one())
                dve.wait_ge(dve_done, own.now())
                d.tensor_tensor(col[:, MNP:MNP + 1], col[:, MNP:MNP + 1], col[:, MN1:MN1 + 1], ALU.min).then_inc(dve_done, own.one())

            def p_plus_q(n, unit, hf):
                dve.wait_ge(pq_loaded[hf], 32 * (n + 1))
                d.scalar_tensor_tensor(pd[:, hf, :], qd[:, hf, :], cols(NE)[:, hf:hf + 1], pd[:, hf, :],
                                       ALU.mult, ALU.add).then_inc(sum_ready, 1)

            def differences(unit, hf):
                L = [logs[:, hf, k, :] for k in range(4)]
                base = 2 + SLOTS * unit
                dve.wait_ge(slot_read, base + 3)
                d.tensor_tensor(L[2], L[2], L[1], ALU.subtract).then_inc(dve_done, own.one())
                dve.wait_ge(slot_read, base + 4)
                d.tensor_tensor(L[3], L[3], L[0], ALU.subtract).then_inc(dve_done, own.one())
                dve.wait_ge(dve_done, own.now())
                dve.wait_ge(low_ready, unit + 1)
                d.tensor_tensor(L[0], L[3], L[2], ALU.subtract).then_inc(dve_done, own.one())
                dve.wait_ge(dve_done, own.now())
                d.scalar_tensor_tensor(L[0], square[:, hf, :], 2.0, L[0], ALU.mult, ALU.add).then_inc(dve_done, own.one())
                dve.wait_ge(dve_done, own.now())
                d.scalar_tensor_tensor(L[1], L[3], 3.0, L[2], ALU.mult, ALU.add, accum_out=col[:, TACC:TACC + 1]
                                       ).then_inc(slopes, 1)
                dve.wait_ge(slopes, unit + 1)
                d.tensor_tensor(cols(ACC)[:, hf:hf + 1], cols(ACC)[:, hf:hf + 1], col[:, TACC:TACC + 1], ALU.add).then_inc(dve_done, own.one())

            def norms(unit, hf):
                L = [logs[:, hf, k, :] for k in range(4)]
                dve.wait_ge(squares, 4 * unit + 2)
                d.tensor_tensor(L[3], L[3], L[2], ALU.add).then_inc(dve_done, own.one())
                dve.wait_ge(squares, 4 * unit + 3)
                dve.wait_ge(dve_done, own.now())
                d.tensor_tensor(L[3], L[3], L[0], ALU.add).then_inc(dve_done, own.one())
                dve.wait_ge(squares, 4 * unit + 4)
                dve.wait_ge(dve_done, own.now())
                d.tensor_tensor(L[3], L[3], square[:, hf, :], ALU.mult).then_inc(z_ready, 1)

            def finish(unit, hf):
                sim = square[:, hf, :]
                dve.wait_ge(inv_ready, unit + 1)
                d.scalar_tensor_tensor(sim, sim, B_NORM, logs[:, hf, 3, :], ALU.mult, ALU.mult).then_inc(dve_done, own.one())
                dve.wait_ge(dve_done, own.now())
                d.tensor_tensor(logs[:, hf, 1, :], logs[:, hf, 1, :], sim, ALU.mult).then_inc(dve_done, own.one())
                dve.wait_ge(dve_done, own.now())
                dve.wait_ge(x1_ready, unit + 1)
                d.tensor_tensor(x1t[:, hf, :], x1t[:, hf, :], logs[:, hf, 1, :], ALU.add).then_inc(dve_done, own.one())
                d.scalar_tensor_tensor(ut[:, hf, :], sim, -1.0, ut[:, hf, :], ALU.add, ALU.mult).then_inc(tail_done, 1)

            def half_chunk(s, i, k, hf, A, Bs, Cs, Ds, first):
                n = 16 * s + 2 * i + k
                nb, nC, nd = n - 16, n - 32, n - 48
                u = 2 * nC + hf
                tail = Cs and not first
                if Ds:
                    p_plus_q(nd, 2 * nd + hf, hf)
                if tail:
                    norms(u - 1, 1 - hf)
                if Bs:
                    copy_h(nb, k, 2 * hf, first, 16 * (8 * (s - 1) + i))
                if Cs:
                    differences(u, hf)
                if Bs:
                    copy_h(nb, k, 2 * hf + 1, first, None)
                    if hf == 1:
                        min_h(k)
                if tail:
                    finish(u - 1, 1 - hf)

            def turn(s, A, Bs, Cs, Ds):
                if Bs:
                    d.memset(mx[:, :], -HUGE).then_inc(dve_done, own.one())
                    d.memset(col[:, MNP:MNP + 1], HUGE).then_inc(dve_done, own.one())
                if Cs:
                    d.memset(cols(ACC), 0.0).then_inc(dve_done, own.one())
                dve.wait_ge(dve_done, own.now())

                def pair(i, first):
                    for k in range(2):
                        for hf in range(2):
                            half_chunk(s, i, k, hf, A, Bs, Cs, Ds, first and k == 0 and hf == 0)
                pair(0, True)
                with own.loop(1, PAIRS, (DVE_MIN_PAIR if Bs else 0) + (DVE_PAIR if Cs else 0)) as i:
                    pair(i, False)
                dve.wait_ge(dve_done, own.now())
                if Cs:
                    u = 32 * (s - 1)
                    norms(u - 1, 1)
                    finish(u - 1, 1)
                    excite(s - 2)
                if Bs:
                    value_range(s - 1)
                if A:
                    stats(s)

            def value_range(b):
                d.tensor_copy(rr[:, 0:1], mx[:, 3:4]).then_inc(dve_done, own.one())
                d.tensor_scalar(rr[:, 1:2], col[:, MNP:MNP + 1], -1.0, None, ALU.mult).then_inc(dve_done, own.one())
                dve.wait_ge(dve_done, own.now())
                d.tensor_copy(mx[:, 0:1], rr[:, 0:1]).then_inc(range_in, 1)
                dve.wait_ge(range_out, b + 1)
                d.scalar_tensor_tensor(col[:, RNG:RNG + 1], rr[:, 2:3], rr[:, 3:4], cst[:, 0:1], ALU.add, ALU.add).then_inc(dve_done, own.one())
                d.tensor_copy(col[:, NEGMIN:NEGMIN + 1], rr[:, 3:4]).then_inc(dve_done, own.one())
                dve.wait_ge(dve_done, own.now())
                d.reciprocal(col[:, INV:INV + 1], col[:, RNG:RNG + 1]).then_inc(dve_done, own.one())
                d.tensor_scalar(cols(XS), cols(RI), col[:, RNG:RNG + 1], None, ALU.mult).then_inc(dve_done, own.one())
                d.tensor_scalar(cols(XK), cols(RI), col[:, NEGMIN:NEGMIN + 1], -1.0, ALU.mult, ALU.mult).then_inc(dve_done, own.one())
                dve.wait_ge(dve_done, own.now())
                d.tensor_tensor(cols(XK), cols(XK), cols(M1), ALU.add).then_inc(dve_done, own.one())
                dve.wait_ge(dve_done, own.now())
                d.tensor_copy(mx[:, 1:2], rr[:, 0:1]).then_inc(range_ready, 1)

            def excite(b):
                dve.wait_ge(dve_done, own.now())
                d.tensor_scalar(gate[:, 0:2], cols(ACC), 1.0 / (SLOPE * PIX), None, ALU.mult).then_inc(sums_ready, 1)
                dve.wait_ge(hidden_ps, b + 1)
                d.tensor_scalar(hid[:, 2:3], o_ps[0:HIDDEN, 0:1], hid[:, 1:2], 0.0, ALU.add, ALU.max
                                ).then_inc(hidden_ready, 1)
                dve.wait_ge(gate_ps, b + 1)
                d.scalar_tensor_tensor(gate[:, 2:4], o_ps[:, 8:10], -1.0, gate[:, 6:8], ALU.mult, ALU.add).then_inc(dve_done, own.one())
                dve.wait_ge(dve_done, own.now())
                d.tensor_scalar(gate[:, 2:4], gate[:, 2:4], EXP_MAX, None, ALU.min).then_inc(gate_arg, 1)
                dve.wait_ge(gate_exp, b + 1)
                d.tensor_scalar(gate[:, 4:6], gate[:, 4:6], 1.0, None, ALU.add).then_inc(dve_done, own.one())
                dve.wait_ge(dve_done, own.now())
                d.reciprocal(cols(NE), gate[:, 4:6]).then_inc(dve_done, own.one())
                dve.wait_ge(dve_done, own.now())
                d.tensor_scalar(cols(NE), cols(NE), -1.0, None, ALU.mult).then_inc(dve_done, own.one())
                dve.wait_ge(dve_done, own.now())

            def rows_of(vectors):
                for k, vec in enumerate(vectors):
                    for h in range(2):
                        d.tensor_scalar(diag[:, 2 * k + h, :], ident[:, :], vec[:, h:h + 1], None, ALU.mult).then_inc(dve_done, own.one())

            def stats(b):
                dve.wait_ge(xa_used, 2 + 2 * CHUNKS * (b + 1))
                d.tensor_copy(gram[:, 0, :], g_ps[:, 0:C]).then_inc(dve_done, own.one())
                d.tensor_copy(gram[:, 1, CH:C], g_ps[:, C + 1:C + 1 + CH]).then_inc(dve_done, own.one())
                d.tensor_copy(col[:, SUM:SUM + 1], g_ps[:, C:C + 1]).then_inc(dve_done, own.one())
                dve.wait_ge(dve_done, own.now())
                d.tensor_copy(col[:, SUM + 1:SUM + 2], g_ps[:, C + 1 + CH:C + 2 + CH]).then_inc(gram_copied, 1)
                dve.wait_ge(gram_turned, b + 1)
                d.tensor_copy(gram[:, 1, 0:CH], xt_ps[:, 0:CH]).then_inc(dve_done, own.one())
                for h in range(2):
                    apart()
                    d.tensor_tensor_reduce(junk, gram[:, h, h * CH:(h + 1) * CH], ident[:, :], 1.0, 0.0,
                                           ALU.mult, ALU.add, col[:, SQ + h:SQ + h + 1]).then_inc(dve_done, own.one())
                    dve.wait_ge(dve_done, own.now())
                d.tensor_copy(junk[:, 0:1], col[:, SQ:SQ + 1]).then_inc(gram_whole, 1)
                dve.wait_ge(group_sums, b + 1)
                d.tensor_scalar(cols(MEAN, 4), h_ps[:, 0:4], 1.0 / PIX, None, ALU.mult).then_inc(dve_done, own.one())
                dve.wait_ge(dve_done, own.now())
                d.tensor_tensor(cols(TMP), cols(MEAN), cols(MEAN), ALU.mult).then_inc(dve_done, own.one())
                dve.wait_ge(dve_done, own.now())
                d.tensor_tensor(cols(VAR), cols(VAR), cols(TMP), ALU.subtract).then_inc(var_ready, 1)
                dve.wait_ge(rs_guess, b + 1)
                d.tensor_scalar(cols(VAR), cols(VAR), GN_EPS, None, ALU.add).then_inc(dve_done, own.one())
                newton(cols(VAR), cols(RS))
                d.tensor_scalar(cols(NMEAN), cols(MEAN), -1.0, None, ALU.mult).then_inc(dve_done, own.one())
                d.scalar_tensor_tensor(cols(WGT), cols(MEAN), float(PIX), cols(SUM), ALU.mult, ALU.subtract).then_inc(dve_done, own.one())
                d.tensor_scalar(cols(GR), cols(RS), col[:, GAM:GAM + 1], None, ALU.mult).then_inc(dve_done, own.one())
                d.scalar_tensor_tensor(cols(DSM), cols(SUM), 1.0 / PIX, cols(MEAN), ALU.mult, ALU.subtract).then_inc(dve_done, own.one())
                d.tensor_scalar(cols(NSP), cols(SUM), -1.0 / PIX, None, ALU.mult).then_inc(dve_done, own.one())
                rows_of((cols(SUM), cols(MEAN), cols(RS)))
                dve.wait_ge(dve_done, own.now())
                d.tensor_scalar(mrep[:, 0, :], ones[:, :], cols(NMEAN)[:, 0:1], None, ALU.mult).then_inc(diag_ready, 1)
                d.tensor_scalar(mrep[:, 1, :], ones[:, :], cols(NMEAN)[:, 1:2], None, ALU.mult).then_inc(dve_done, own.one())
                dve.wait_ge(rows_ready, b + 1)
                d.tensor_copy(rows[:, 0:2, :].rearrange("p k c -> p (k c)"), xt_ps[:, :]).then_inc(dve_done, own.one())
                d.tensor_copy(rows[:, 2, :], h_ps[:, 256:512]).then_inc(dve_done, own.one())
                dve.wait_ge(dve_done, own.now())
                for h in range(2):
                    d.scalar_tensor_tensor(attn[:, h, :], rows[:, 0, :], cols(NMEAN)[:, h:h + 1], gram[:, h, :],
                                           ALU.mult, ALU.add).then_inc(dve_done, own.one())
                dve.wait_ge(dve_done, own.now())
                for h in range(2):
                    d.scalar_tensor_tensor(attn[:, h, :], rows[:, 1, :], cols(WGT)[:, h:h + 1], attn[:, h, :],
                                           ALU.mult, ALU.add).then_inc(dve_done, own.one())
                dve.wait_ge(dve_done, own.now())
                for h in range(2):
                    d.scalar_tensor_tensor(attn[:, h, :], attn[:, h, :], cols(RS)[:, h:h + 1], rows[:, 2, :],
                                           ALU.mult, ALU.mult).then_inc(dve_done, own.one())
                dve.wait_ge(dve_done, own.now())
                for h in range(2):
                    d.tensor_reduce(cols(NMAX)[:, h:h + 1], attn[:, h, :], AX_X, ALU.max).then_inc(dve_done, own.one())
                dve.wait_ge(dve_done, own.now())
                d.tensor_scalar(cols(NMAX), cols(NMAX), -1.0, None, ALU.mult).then_inc(logits_ready, 1)
                dve.wait_ge(exp_ready, b + 1)
                d.reciprocal(cols(ESUM), cols(ESUM)).then_inc(dve_done, own.one())
                dve.wait_ge(dve_done, own.now())
                d.tensor_tensor(cols(GR), cols(GR), cols(ESUM), ALU.mult).then_inc(dve_done, own.one())
                dve.wait_ge(dve_done, own.now())
                for h in range(2):
                    d.tensor_scalar(step[:, h, :], attn[:, h, :], cols(GR)[:, h:h + 1], None, ALU.mult).then_inc(dve_done, own.one())
                dve.wait_ge(dve_done, own.now())
                for h in range(2):
                    at = step[:, h, h * CH:(h + 1) * CH]
                    d.tensor_tensor(at, at, diag[:, 4 + h, :], ALU.add).then_inc(dve_done, own.one())
                dve.wait_ge(dve_done, own.now())
                for h in range(2):
                    d.tensor_copy(full[:, h, :], step[:, h, :]).then_inc(dve_done, own.one())
                dve.wait_ge(dve_done, own.now())
                for h in range(2):
                    at = full[:, h, h * CH:(h + 1) * CH]
                    d.tensor_tensor(at, at, ident[:, :], ALU.add).then_inc(dve_done, own.one())
                dve.wait_ge(dve_done, own.now())
                d.tensor_copy(junk[:, 0:1], col[:, SQ:SQ + 1]).then_inc(step_ready, 1)
                d.scalar_tensor_tensor(gramc[:, 0, :], rows[:, 0, :], cols(NSP)[:, 0:1], gram[:, 0, :], ALU.mult, ALU.add).then_inc(dve_done, own.one())
                dve.wait_ge(dve_done, own.now())
                d.scalar_tensor_tensor(gramc[:, 1, :], rows[:, 0, :], cols(NSP)[:, 1:2], gram[:, 1, :], ALU.mult, ALU.add
                                       ).then_inc(gramc_ready, 1)
                dve.wait_ge(cov_ready, b + 1)
                d.tensor_tensor(prod[:, 0, :], full[:, 0, :], o_ps[:, 0:C], ALU.mult).then_inc(dve_done, own.one())
                dve.wait_ge(dve_done, own.now())
                d.tensor_tensor(prod[:, 1, :], full[:, 1, :], o_ps[:, C:2 * C], ALU.mult).then_inc(prod_ready, 1)
                dve.wait_ge(mean_ready, b + 1)
                d.tensor_tensor(cols(MU), xt_ps[:, 0:2], cols(NSP), ALU.subtract).then_inc(dve_done, own.one())
                dve.wait_ge(dve_done, own.now())
                d.tensor_tensor(cols(M2), cols(MU), cols(MU), ALU.mult).then_inc(dve_done, own.one())
                dve.wait_ge(dve_done, own.now())
                dve.wait_ge(var1_sums, b + 1)
                d.scalar_tensor_tensor(cols(M2), g_ps[:, 8:10], 1.0 / PIX, cols(M2), ALU.mult, ALU.add).then_inc(mom_ready, 1)
                dve.wait_ge(mom_group, b + 1)
                d.tensor_copy(cols(M1, 4), g_ps[:, 16:20]).then_inc(dve_done, own.one())
                dve.wait_ge(dve_done, own.now())
                d.tensor_tensor(cols(TMP), cols(M1), cols(M1), ALU.mult).then_inc(dve_done, own.one())
                dve.wait_ge(dve_done, own.now())
                d.tensor_tensor(cols(V1), cols(V1), cols(TMP), ALU.subtract).then_inc(var1_ready, 1)
                dve.wait_ge(rs1_guess, b + 1)
                d.tensor_scalar(cols(V1), cols(V1), GN_EPS, None, ALU.add).then_inc(dve_done, own.one())
                newton(cols(V1), cols(R1))
                d.tensor_tensor(cols(RI), cols(V1), cols(R1), ALU.mult).then_inc(dve_done, own.one())
                rows_of((cols(R1), cols(M1)))
                dve.wait_ge(dve_done, own.now())
                d.tensor_copy(junk[:, 0:1], col[:, SQ:SQ + 1]).then_inc(diag1_ready, 1)
                dve.wait_ge(rows1_ready, b + 1)
                d.tensor_copy(rows[:, 0:2, :].rearrange("p k c -> p (k c)"), o_ps[:, :]).then_inc(dve_done, own.one())
                d.tensor_copy(rows[:, 2, :], h_ps[:, 0:C]).then_inc(dve_done, own.one())
                dve.wait_ge(dve_done, own.now())
                for h in range(2):
                    d.tensor_tensor(mix[:, h, :], full[:, h, :], rows[:, 0, :], ALU.mult).then_inc(dve_done, own.one())
                d.tensor_tensor(rows[:, 2, :], rows[:, 2, :], rows[:, 1, :], ALU.subtract).then_inc(dve_done, own.one())
                dve.wait_ge(dve_done, own.now())
                d.tensor_tensor(shift[:, 0, :], rows[:, 2, :], rows[:, 0, :], ALU.mult).then_inc(dve_done, own.one())
                dve.wait_ge(dve_done, own.now())
                d.tensor_copy(shift[:, 1, :], shift[:, 0, :]).then_inc(mix_ready, 1)

            images(lambda lo, hi: own.loop(lo, hi, DVE_IMAGE), turn)


_INS = ['x', 'L0_conv_gamma', 'L1_conv_w1', 'L1_conv_b1', 'L1_conv_w2', 'L1_conv_b2', 'L1_conv_gamma',
        'L1_conv_beta', 'L1_conv_moving_mean', 'L1_conv_moving_var']
_OUTS = [((B, H, W, C), 'float32')]


def kernel(**inputs):
    import numpy as _np
    import concourse.bacc as _bacc
    from concourse import mybir as _mybir
    from concourse.bass_utils import run_bass_kernel_spmd as _run

    nc = _bacc.Bacc("TRN2", target_bir_lowering=False, num_devices=1)
    arrays, args = {}, []
    for name in _INS:
        a = _np.ascontiguousarray(inputs[name])
        arrays[f"in_{name}_dram"] = a
        args.append(nc.dram_tensor(f"in_{name}_dram", a.shape, _mybir.dt.from_np(a.dtype), kind="ExternalInput").ap())
    for i, (shape, dtype) in enumerate(_OUTS):
        dt = _mybir.dt.from_np(_np.dtype(dtype))
        args.append(nc.dram_tensor(f"out_{i}_dram", shape, dt, kind="ExternalOutput").ap())
    mk_conv_preact(nc, *args)
    r = _run(nc, [arrays], core_ids=[0])
    got = tuple(r.results[0][f"out_{i}_dram"] for i in range(len(_OUTS)))
    return got[0]
```

```python
import math
from contextlib import ExitStack, contextmanager

import concourse.bass as bass
from concourse import mybir

F32 = mybir.dt.float32
ALU = mybir.AluOpType
ACT = mybir.ActivationFunctionType
AX_X = mybir.AxisListType.X
RMAX = bass.bass_isa.ReduceOp.max

B, H, W, C = 8, 128, 128, 256
CH = C // 2
PIX = H * W
ROWS = 8
CHUNKS = H // ROWS
PAIRS = CHUNKS // 2
SUB = 4
UNIT = ROWS * W
HIDDEN = C // 8
GROUP = C // 32
SCALES = (2, 4, 8, 16)
SLOTS = len(SCALES) + 1
GN_EPS = 1e-5
BN_EPS = 1e-3
EPS = 1e-7
LN2 = math.log(2.0)
SLOPE = -LN2
LINEAR_SCALE = math.sqrt(5.0)
QUAD_SCALE = 0.5
CUBIC_SCALE = math.sqrt(1.0 / 20.0)
TINY = 1e-37
HUGE = 3.0e38
EXP_MAX = 85.0

POOL_CONST = 10 + 1 + 2 * len(SCALES) + 2
POOL_PAIR, POOL_IMAGE = 6, 53
ACT_PAIR, ACT_IMAGE = 24, 196
DVE_MIN_PAIR, DVE_PAIR, DVE_IMAGE = 4, 32, 370


class Count:

    def __init__(self, eng, sem):
        self.eng, self.sem, self.base, self.k, self.total = eng, sem, 0, 0, 0

    def one(self):
        self.k += 1
        self.total += 1
        return 1

    def now(self):
        return self.base + self.k

    @contextmanager
    def loop(self, start, stop, per_turn):
        entry, before = self.base + self.k, self.total
        with self.eng.Fori(start, stop) as i:
            self.base, self.k = entry + per_turn * (i - start), 0
            yield i
            assert self.total - before == per_turn, (self.sem, self.total - before, per_turn)
        self.base, self.k = entry, per_turn * (stop - start)
        self.total = before + per_turn * (stop - start)


def some(count):
    return not (isinstance(count, int) and count <= 0)


def mk_conv_preact(nc, x, gamma, w1, b1, w2, b2, bn_gamma, bn_beta, bn_mean, bn_var, out):
    with ExitStack() as ctx:
        def sb(name, shape, dt=F32):
            return ctx.enter_context(nc.sbuf_tensor(name, shape, dt))

        def sem(name):
            return ctx.enter_context(nc.semaphore(name))

        h_dram = nc.dram_tensor("h_scratch", (B * CHUNKS, W, ROWS * C), F32, kind="Internal").ap()
        p_dram = nc.dram_tensor("p_scratch", (B * CHUNKS * 2, CH, UNIT), F32, kind="Internal").ap()
        q_dram = nc.dram_tensor("q_scratch", (B * CHUNKS * 2, CH, UNIT), F32, kind="Internal").ap()
        x_sub = x.rearrange("b (n h) w c -> (b n) w h c", h=SUB)
        out_chunk = out.rearrange("b (n h) w c -> (b n) w h c", h=ROWS)

        xa = sb("xa", [W, 2, SUB, C + 1])
        xb = sb("xb", [W, 2, SUB, C])
        xt = sb("xt", [CH, 2, 2, 2, W])
        h_out = sb("h_out", [W, 2, ROWS, C])
        h_in = sb("h_in", [W, ROWS, C])
        v = sb("v", [W, 2, 2 * ROWS, CH])
        t2 = sb("t2", [W, 2, 2 * ROWS, CH])
        t4 = sb("t4", [W, 2, 2 * ROWS, CH])
        t8 = sb("t8", [W, 2, 2 * ROWS, CH])
        logs = sb("logs", [CH, 2, 4, UNIT])
        square = sb("square", [CH, 2, UNIT])
        ut = sb("ut", [CH, 2, UNIT])
        x1t = sb("x1t", [CH, 2, UNIT])
        pd = sb("pd", [CH, 2, UNIT])
        qd = sb("qd", [CH, 2, UNIT])
        o_sb = sb("o_sb", [W, 2, ROWS, C])

        ident = sb("ident", [128, 128])
        ones = sb("ones", [128, 128])
        zeros = sb("zeros", [128, 128])
        band = sb("band", [W, 4, W])
        group = sb("group", [128, 128])
        mix = sb("mix", [CH, 2, C])
        shift = sb("shift", [128, 2, C])
        col = sb("col", [128, 64])
        w1s = sb("w1s", [CH, 2, HIDDEN])
        w2s = sb("w2s", [HIDDEN, C])
        hid = sb("hid", [HIDDEN, 4])
        prm = sb("prm", [CH, 5, 2])

        in_xt = xt[:, :, :, :, :].rearrange("p a j r w -> p (a j r w)")
        gram = in_xt[:, 0:512].rearrange("p (h c) -> p h c", h=2)
        attn = in_xt[:, 512:1024].rearrange("p (h c) -> p h c", h=2)
        in_h0, in_h1 = (h_out[:, k, :, :].rearrange("p r c -> p (r c)") for k in range(2))
        diag = in_h0[:, 0:768].rearrange("p (k c) -> p k c", k=6)
        rows = in_h0[:, 768:1536].rearrange("p (k c) -> p k c", k=3)
        mrep = in_h0[:, 1536:1792].rearrange("p (h c) -> p h c", h=2)
        junk = in_h0[:, 1792:1920]
        step = in_h1[:, 0:512].rearrange("p (h c) -> p h c", h=2)
        full = in_h1[:, 512:1024].rearrange("p (h c) -> p h c", h=2)
        gramc = in_h1[:, 1024:1536].rearrange("p (h c) -> p h c", h=2)
        prod = in_h1[:, 1536:2048].rearrange("p (h c) -> p h c", h=2)

        def cols(at, n=2):
            return col[:, at:at + n]
        (SUM, SQ, MEAN, VAR, RS, TMP, NMEAN, WGT, NMAX, ESUM, GR, DSM, MU, M2, M1, V1, R1, RI, NSP) = range(0, 38, 2)
        GAM, HMAX, HMIN, MX, MNP, RNG, INV, NEGMIN = 38, 39, 40, 41, 45, 46, 47, 48
        XS, XK, GS, GB, NE, ACC, TACC = 49, 51, 53, 55, 57, 59, 61
        cst = sb("cst", [128, 4])
        C_EPS, C_TINY, C_ONE, C_GN = range(4)
        gate = sb("gate", [128, 8])
        mx = sb("mx", [128, 4])
        mins = sb("mins", [128, 2 * CHUNKS])
        rr = sb("rr", [128, 4])

        def bank(name, n=1):
            return ctx.enter_context(nc.psum_tensor(name, [128, n * 512], F32))
        g_ps = bank("g_ps")
        xt_ps = bank("xt_ps")
        h_ps = bank("h_ps")
        o_ps = bank("o_ps")
        slot = [bank("slot0", 2), bank("slot1", 2)]

        const_loaded = sem("const_loaded")
        pool_const = sem("pool_const")
        const_ready = sem("const_ready")
        xa_loaded = [sem("xa_loaded0"), sem("xa_loaded1")]
        xb_loaded = [sem("xb_loaded0"), sem("xb_loaded1")]
        xa_used = sem("xa_used")
        xt_filled = sem("xt_filled")
        xt_copied = sem("xt_copied")
        h_filled = sem("h_filled")
        h_copied = sem("h_copied")
        h_stored = [sem("h_stored0"), sem("h_stored1")]
        h_loaded = sem("h_loaded")
        v_done = sem("v_done")
        t_ready = {2: sem("t2_ready"), 4: sem("t4_ready"), 8: sem("t8_ready")}
        slot_filled = sem("slot_filled")
        slot_read = sem("slot_read")
        slopes = sem("slopes")
        squares = sem("squares")
        low_ready = sem("low_ready")
        high_ready = sem("high_ready")
        quad_ready = sem("quad_ready")
        z_ready = sem("z_ready")
        inv_ready = sem("inv_ready")
        x1_ready = sem("x1_ready")
        sig_used = sem("sig_used")
        tail_done = sem("tail_done")
        pq_stored = [sem("pq_stored0"), sem("pq_stored1")]
        pq_loaded = [sem("pq_loaded0"), sem("pq_loaded1")]
        sum_ready = sem("sum_ready")
        o_filled = sem("o_filled")
        o_copied = sem("o_copied")
        o_stored = [sem("o_stored0"), sem("o_stored1")]
        dve_done = sem("dve_done")
        act_done = sem("act_done")
        pool_done = sem("pool_done")
        pool_apart, dve_apart, sp_apart = sem("pool_apart"), sem("dve_apart"), sem("sp_apart")
        gram_copied = sem("gram_copied"); gram_turned = sem("gram_turned"); gram_whole = sem("gram_whole")
        group_sums = sem("group_sums"); var_ready = sem("var_ready"); rs_guess = sem("rs_guess")
        diag_ready = sem("diag_ready"); rows_ready = sem("rows_ready"); logits_ready = sem("logits_ready")
        exp_ready = sem("exp_ready"); step_ready = sem("step_ready"); mean_ready = sem("mean_ready")
        gramc_ready = sem("gramc_ready"); cov_ready = sem("cov_ready"); prod_ready = sem("prod_ready")
        var1_sums = sem("var1_sums"); mom_ready = sem("mom_ready"); mom_group = sem("mom_group")
        var1_ready = sem("var1_ready"); rs1_guess = sem("rs1_guess"); diag1_ready = sem("diag1_ready")
        rows1_ready = sem("rows1_ready"); mix_ready = sem("mix_ready")
        range_in = sem("range_in"); range_out = sem("range_out"); range_ready = sem("range_ready")
        sums_ready = sem("sums_ready"); hidden_ps = sem("hidden_ps"); hidden_ready = sem("hidden_ready")
        gate_ps = sem("gate_ps"); gate_arg = sem("gate_arg"); gate_exp = sem("gate_exp")
        bn_logs = sem("bn_logs")

        block = ctx.enter_context(nc.Block())

        def images(loop, turn):
            for s in range(3):
                turn(s, True, s >= 1, s >= 2, False)
            with loop(3, B) as s:
                turn(s, True, True, True, True)
            for s in range(B, B + 3):
                turn(s, False, s <= B, s <= B + 1, True)

        @block.sync
        def _(sp):
            def apart():
                sp.sem_inc(sp_apart, 1)

            for dst, src in ((w1s[:, :, :], w1.rearrange("(h c) r -> c h r", h=2)), (w2s[:, :], w2),
                             (hid[:, 0:1], b1.rearrange("(r o) -> r o", o=1)),
                             (col[:, GAM:GAM + 1], gamma.rearrange("(a o) -> a o", o=1).to_broadcast([128, 1]))):
                sp.dma_start(dst, src).then_inc(const_loaded, 16)
            with nc.allow_non_contiguous_dma(reason="five short parameter columns"):
                for k, src in enumerate((bn_gamma, bn_beta, bn_mean, bn_var, b2)):
                    sp.dma_start(prm[:, k, :], src.rearrange("(h c) -> c h", h=2)).then_inc(const_loaded, 16)

            def chunk(s, i, k, A, Bs, Cs, Ds, first, last):
                c = 2 * i + k
                n = 16 * s + c
                nb, nC, nd = n - 16, n - 32, n - 48
                prev = not (first and k == 0)
                for hf in range(2):
                    if Cs and hf == 0 and not (last and k == 1):
                        sp.wait_ge(v_done, 2 * (nC + 1))
                        apart()
                        sp.dma_start(h_in[:, :, :].rearrange("p r c -> p (r c)"),
                                     h_dram[nC + 1]).then_inc(h_loaded, 16)
                    if A:
                        sp.wait_ge(xa_used, 2 * n + hf + 1)
                        apart()
                        sp.dma_start(xa[:, hf, :, 0:C], x_sub[2 * n + hf]).then_inc(xa_loaded[hf], 16)
                    if Bs:
                        if some(4 * nb + 2 * hf):
                            sp.wait_ge(xt_filled, 4 * nb + 2 * hf)
                        apart()
                        sp.dma_start(xb[:, hf, :, :], x_sub[2 * nb + hf]).then_inc(xb_loaded[hf], 16)
                    if Ds and first and k == 0 and hf == 0:
                        for left in (2, 1):
                            store_pq(2 * (nd + 16) - left, left % 2)
                        for p in pq_stored:
                            sp.wait_ge(p, 32 * CHUNKS * (s - 2))
                            apart()
                    if Ds:
                        sp.wait_ge(o_filled, 2 * (2 * nd + hf))
                        apart()
                        sp.dma_start(pd[:, hf, :], p_dram[2 * nd + hf]).then_inc(pq_loaded[hf], 16)
                        sp.dma_start(qd[:, hf, :], q_dram[2 * nd + hf]).then_inc(pq_loaded[hf], 16)
                    if Cs and hf == 0 and not first:
                        store_pq(2 * nC - 3, 1)
                    if Cs and hf == 1 and prev:
                        store_pq(2 * nC - 2, 0)
                    if Bs and hf == 1 and prev:
                        sp.wait_ge(h_copied, 4 * nb + 1)
                        apart()
                        sp.dma_start(h_dram[nb - 1], h_out[:, 1 - k, :, :].rearrange("p r c -> p (r c)")
                                     ).then_inc(h_stored[1 - k], 16)
                    if Ds and hf == 1 and prev:
                        sp.wait_ge(o_copied, 4 * nd + 1)
                        apart()
                        sp.dma_start(out_chunk[nd - 1], o_sb[:, 1 - k, :, :]).then_inc(o_stored[1 - k], 16)

            def store_pq(unit, hf):
                sp.wait_ge(tail_done, unit + 3)
                apart()
                sp.dma_start(p_dram[unit], x1t[:, hf, :]).then_inc(pq_stored[hf], 16)
                sp.dma_start(q_dram[unit], ut[:, hf, :]).then_inc(pq_stored[hf], 16)

            def turn(s, A, Bs, Cs, Ds):
                if Cs:
                    for p in h_stored:
                        sp.wait_ge(p, 16 * PAIRS * (s - 1))
                        apart()
                    if some(32 * (s - 2)):
                        sp.wait_ge(v_done, 32 * (s - 2))
                    apart()
                    sp.dma_start(h_in[:, :, :].rearrange("p r c -> p (r c)"),
                                 h_dram[16 * (s - 2)]).then_inc(h_loaded, 16)

                def pair(i, first, last):
                    for k in range(2):
                        chunk(s, i, k, A, Bs, Cs, Ds, first, last)
                pair(0, True, False)
                with sp.Fori(1, PAIRS - 1) as i:
                    pair(i, False, False)
                pair(PAIRS - 1, False, True)
                n = 16 * (s + 1)
                if Cs:
                    store_pq(2 * (n - 32) - 3, 1)
                if Bs:
                    sp.wait_ge(h_copied, 4 * (n - 16) + 1)
                    apart()
                    sp.dma_start(h_dram[n - 17], h_out[:, 1, :, :].rearrange("p r c -> p (r c)")
                                 ).then_inc(h_stored[1], 16)
                if Ds:
                    sp.wait_ge(o_copied, 4 * (n - 48) + 1)
                    apart()
                    sp.dma_start(out_chunk[n - 49], o_sb[:, 1, :, :]).then_inc(o_stored[1], 16)

            images(sp.Fori, turn)
            for p in o_stored:
                sp.wait_ge(p, 16 * PAIRS * B)
                apart()

        @block.gpsimd
        def _(pool):
            g = nc.gpsimd
            g.memset(ident[:, :], 0.0).then_inc(pool_const, 1)
            g.memset(ones[:, :], 1.0).then_inc(pool_const, 1)
            g.memset(band[:, :, :], 1.0).then_inc(pool_const, 1)
            g.memset(group[:, :], 1.0 / GROUP).then_inc(pool_const, 1)
            g.memset(xa[:, :, :, C:C + 1], 1.0).then_inc(pool_const, 1)
            for j, value in enumerate((EPS, TINY, 1.0, GN_EPS)):
                g.memset(cst[:, j:j + 1], value).then_inc(pool_const, 1)
            g.memset(mx[:, :], -HUGE).then_inc(pool_const, 1)
            pool.wait_ge(pool_const, 10)
            made = 10
            g.affine_select(out=ident[:, :], in_=ident[:, :], compare_op=ALU.not_equal, fill=1.0, base=0,
                            pattern=[[-1, 128]], channel_multiplier=1).then_inc(pool_const, 1)
            for k, size in enumerate(SCALES):
                lo = (size - 1) // 2
                hi = size - 1 - lo
                pool.wait_ge(pool_const, made + 1)
                g.affine_select(out=band[:, k, :], in_=band[:, k, :], compare_op=ALU.is_ge, fill=0.0, base=lo,
                                pattern=[[-1, W]], channel_multiplier=1).then_inc(pool_const, 1)
                pool.wait_ge(pool_const, made + 2)
                g.affine_select(out=band[:, k, :], in_=band[:, k, :], compare_op=ALU.is_ge, fill=0.0, base=hi,
                                pattern=[[1, W]], channel_multiplier=-1).then_inc(pool_const, 1)
                made += 2
            gv = group[:, :].rearrange("p (g c) -> p g c", c=GROUP)
            pool.wait_ge(pool_const, made + 1)
            g.affine_select(out=gv, in_=gv, compare_op=ALU.is_ge, fill=0.0, base=0,
                            pattern=[[-GROUP, 128 // GROUP], [0, GROUP]], channel_multiplier=1).then_inc(pool_const, 1)
            pool.wait_ge(pool_const, made + 2)
            g.affine_select(out=gv, in_=gv, compare_op=ALU.is_ge, fill=0.0, base=GROUP - 1,
                            pattern=[[GROUP, 128 // GROUP], [0, GROUP]], channel_multiplier=-1).then_inc(pool_const, 1)
            assert made + 3 == POOL_CONST
            own = Count(pool, pool_done)

            def apart():
                pool.sem_inc(pool_apart, 1)

            def add_rows(dst, src, hf, k, gap):
                a = k * ROWS
                if k == 1:
                    parts = [(a, a - gap, ROWS)]
                else:
                    parts = [(a, 2 * ROWS - gap, gap), (a + gap, a, ROWS - gap)]
                for d, e, n in parts:
                    ins = g.tensor_tensor(dst[:, hf, d:d + n, :], src[:, hf, d:d + n, :], src[:, hf, e:e + n, :], ALU.add)
                    if (d, e, n) == parts[-1]:
                        ins.then_inc(t_ready[2 * gap], 1)
                    else:
                        ins.then_inc(pool_done, own.one())

            def new_rows(k, hf, load):
                a = k * ROWS
                if load is None:
                    apart()
                    g.memset(v[:, hf, a:a + ROWS, :], 0.0).then_inc(pool_done, own.one())
                    pool.wait_ge(pool_done, own.now())
                else:
                    pool.wait_ge(h_loaded, 16 * (load + 1))
                    apart()
                    g.tensor_scalar(v[:, hf, a:a + ROWS, :], h_in[:, :, hf * CH:(hf + 1) * CH],
                                    col[:, NEGMIN:NEGMIN + 1], col[:, INV:INV + 1], ALU.add, ALU.mult).then_inc(v_done, 1)
                    pool.wait_ge(v_done, 2 * load + hf + 1)
                add_rows(t2, v, hf, k, 1)

            def more_row_sums(k, hf, count):
                pool.wait_ge(pool_done, own.now())
                pool.wait_ge(t_ready[2], count)
                add_rows(t4, t2, hf, k, 2)
                pool.wait_ge(pool_done, own.now())
                pool.wait_ge(t_ready[4], count)
                add_rows(t8, t4, hf, k, 4)

            def low_contrast(unit, hf):
                pool.wait_ge(tail_done, unit + 1)
                pool.wait_ge(slot_read, 2 + SLOTS * unit + 2)
                g.tensor_tensor(square[:, hf, :], logs[:, hf, 0, :], logs[:, hf, 1, :], ALU.subtract).then_inc(low_ready, 1)

            def quad_contrast(unit, hf):
                pool.wait_ge(low_ready, unit + 1)
                pool.wait_ge(high_ready, unit + 1)
                g.tensor_tensor(logs[:, hf, 0, :], square[:, hf, :], logs[:, hf, 3, :], ALU.subtract).then_inc(quad_ready, 1)

            def make_x1(unit, hf):
                pool.wait_ge(slot_read, 2 + SLOTS * unit + SLOTS)
                apart()
                g.tensor_scalar(x1t[:, hf, :], ut[:, hf, :], col[:, XS + hf:XS + hf + 1], col[:, XK + hf:XK + hf + 1],
                                ALU.mult, ALU.add).then_inc(x1_ready, 1)

            def turn(s, A, Bs, Cs, Ds):
                image = s - 2
                if Cs:
                    pool.wait_ge(range_ready, s - 1)
                    if not (isinstance(s, int) and s == 2):
                        pool.wait_ge(slot_filled, SLOTS * 32 * image)
                    apart()
                    g.memset(v[:, :, ROWS - 1:ROWS, :], 0.0).then_inc(pool_done, own.one())
                    g.memset(t2[:, :, ROWS - 2:ROWS, :], 0.0).then_inc(pool_done, own.one())
                    g.memset(t4[:, :, ROWS - 4:ROWS, :], 0.0).then_inc(pool_done, own.one())
                    pool.wait_ge(pool_done, own.now())
                    for hf in range(2):
                        new_rows(1, hf, 16 * image)
                        more_row_sums(1, hf, 34 * image + hf + 1)

                    def pair(i, first, last):
                        for k in range(2):
                            n = 16 * image + 2 * i + k
                            for hf in range(2):
                                unit = 2 * n + hf
                                before = not (first and k == 0 and hf == 0)
                                if not (first and k == 0):
                                    make_x1(unit - 2, hf)
                                    pool.wait_ge(slot_filled, SLOTS * (unit - 1))
                                new_rows(k, hf, None if last and k == 1 else n + 1)
                                if before:
                                    low_contrast(unit - 1, 1 - hf)
                                more_row_sums(k, hf, unit + 3 + 2 * image)
                                if before:
                                    quad_contrast(unit - 1, 1 - hf)
                    pair(0, True, False)
                    with own.loop(1, PAIRS - 1, POOL_PAIR) as i:
                        pair(i, False, False)
                    pair(PAIRS - 1, False, True)
                    end = 32 * (image + 1)
                    make_x1(end - 2, 0)
                    low_contrast(end - 1, 1)
                    quad_contrast(end - 1, 1)
                    make_x1(end - 1, 1)
                if Bs:
                    pool.wait_ge(range_in, s)
                    apart()
                    g.partition_all_reduce(rr[:, 2:4], rr[:, 0:2], 128, RMAX).then_inc(range_out, 1)

            images(lambda lo, hi: own.loop(lo, hi, POOL_IMAGE), turn)

        @block.tensor
        def _(pe):
            t = nc.tensor
            pe.sem_inc(xa_used, 2)
            pe.sem_inc(xt_filled, 2)
            pe.sem_inc(h_filled, 2)
            pe.sem_inc(o_filled, 2)
            pe.wait_ge(const_ready, 1)

            def gram_rows(n, hf, half):
                if half == 0:
                    pe.wait_ge(xa_loaded[hf], 16 * (n + 1))
                for r in (2 * half, 2 * half + 1):
                    xr = xa[:, hf, r, :]
                    t.matmul(g_ps[:, 0:C + 1], xr[:, 0:CH], xr[:, :], start=False, stop=False, skip_group_check=True)
                    ins = t.matmul(g_ps[:, C + 1:C + 2 + CH], xr[:, CH:C], xr[:, CH:C + 1], start=False, stop=False,
                                   skip_group_check=True)
                if half == 1:
                    ins.then_inc(xa_used, 1)

            def turn_x(n, q):
                m = 4 * n + q
                if q % 2 == 0:
                    pe.wait_ge(xb_loaded[q // 2], 16 * (n + 1))
                pe.wait_ge(xt_copied, m + 1)
                for jh in range(2):
                    for r in range(2):
                        ins = t.transpose(xt_ps[:, (2 * jh + r) * W:(2 * jh + r + 1) * W],
                                          xb[:, q // 2, 2 * (q % 2) + r, jh * CH:(jh + 1) * CH], ident[:, :])
                ins.then_inc(xt_filled, 1)

            def mix_x(n, q):
                m = 4 * n + q
                pe.wait_ge(xt_copied, m + 2)
                pe.wait_ge(h_copied, m + 1)
                for r in range(2):
                    for jh in range(2):
                        ins = t.matmul(h_ps[:, r * C:(r + 1) * C], xt[:, q % 2, jh, r, :], mix[:, jh, :],
                                       start=(jh == 0), stop=(jh == 1))
                ins.then_inc(h_filled, 1)

            def box(unit, k, hf, which):
                s = SLOTS * unit + which
                if which < 3:
                    pe.wait_ge(t_ready[SCALES[which]], unit + 3 + 2 * image_of[0])
                pe.wait_ge(slot_read, s + 1)
                dst = slot[(hf + which) % 2]
                new, old = k * ROWS, (1 - k) * ROWS
                for j in range(ROWS):
                    o = dst[:, j * W:(j + 1) * W]
                    if which == 4:
                        ins = t.transpose(o, v[:, hf, old + j, :], ident[:, :])
                        continue
                    src, lag = ((t2, 1), (t4, 2), (t8, 4), (t8, 0))[which]
                    at = old + lag + j if lag + j < ROWS else new + lag + j - ROWS
                    ins = t.matmul(o, src[:, hf, at, :], band[:, which, :], start=True, stop=(which < 3))
                    if which == 3:
                        ins = t.matmul(o, t8[:, hf, new + j, :], band[:, which, :], start=False, stop=True)
                ins.then_inc(slot_filled, 1)

            def turn_back(unit, hf, d):
                if d == 0:
                    pe.wait_ge(sum_ready, unit + 1)
                pe.wait_ge(o_copied, 2 * unit + d + 1)
                for r in range(4):
                    ins = t.transpose(o_ps[:, r * CH:(r + 1) * CH], pd[:, hf, (4 * d + r) * W:(4 * d + r + 1) * W],
                                      ident[:, :])
                ins.then_inc(o_filled, 1)

            def half_chunk(n, i, k, hf, A, Bs, Cs, Ds):
                nb, nC, nd = n - 16, n - 32, n - 48
                u = 2 * nC + hf
                if Cs:
                    box(u, k, hf, 0)
                    box(u, k, hf, 1)
                if Bs:
                    turn_x(nb, 2 * hf)
                if A:
                    gram_rows(n, hf, 0)
                if Cs:
                    box(u, k, hf, 2)
                if Bs and k == 0 and hf == 0:
                    pe.wait_ge(mix_ready, image_of[0] + 2)
                if Bs:
                    mix_x(nb, 2 * hf)
                    turn_x(nb, 2 * hf + 1)
                if Cs:
                    box(u, k, hf, 3)
                if Ds:
                    turn_back(2 * nd + hf, hf, 0)
                if Cs:
                    box(u, k, hf, 4)
                if A:
                    gram_rows(n, hf, 1)
                if Bs:
                    mix_x(nb, 2 * hf + 1)
                if Ds:
                    turn_back(2 * nd + hf, hf, 1)

            image_of = [None]

            def turn(s, A, Bs, Cs, Ds):
                image_of[0] = s - 2
                if A:
                    if not (isinstance(s, int) and s == 0):
                        pe.wait_ge(gram_copied, s)
                    t.matmul(g_ps[:, :], zeros[:, :], band[:, :, :].rearrange("p k w -> p (k w)"), start=True, stop=False, skip_group_check=True)
                def pair(i):
                    for k in range(2):
                        for hf in range(2):
                            half_chunk(16 * s + 2 * i + k, i, k, hf, A, Bs, Cs, Ds)
                with pe.Fori(0, PAIRS) as i:
                    pair(i)
                if Ds:
                    pe.wait_ge(o_copied, 64 * (s - 2) + 1)
                if A:
                    stats_to_covariance(s)
                if Cs:
                    excite_hidden(s - 2)
                if A:
                    stats_variance(s)
                if Cs:
                    excite_gate(s - 2)
                if A:
                    stats_moments(s)

            def excite_hidden(b):
                pe.wait_ge(sums_ready, b + 1)
                for h in range(2):
                    ins = t.matmul(xt_ps[0:HIDDEN, 256:257], w1s[:, h, :], gate[:, h:h + 1], start=(h == 0), stop=(h == 1))
                ins.then_inc(hidden_ps, 1)

            def excite_gate(b):
                pe.wait_ge(hidden_ready, b + 1)
                for h in range(2):
                    ins = t.matmul(xt_ps[:, 264 + h:265 + h], w2s[:, h * CH:(h + 1) * CH], hid[:, 2:3], start=True, stop=True)
                ins.then_inc(gate_ps, 1)

            def stats_to_covariance(b):
                pe.wait_ge(gram_copied, b + 1)
                t.transpose(xt_ps[:, 0:CH], gram[:, 0, CH:C], ident[:, :]).then_inc(gram_turned, 1)
                pe.wait_ge(gram_whole, b + 1)
                t.matmul(h_ps[:, 0:4], group[:, :], cols(SUM, 4), start=True, stop=True).then_inc(group_sums, 1)
                pe.wait_ge(diag_ready, b + 1)
                for k in range(4):
                    t.matmul(xt_ps[:, k * 128:(k + 1) * 128], ones[:, :], diag[:, k, :], start=True, stop=True)
                for k in range(2):
                    ins = t.matmul(h_ps[:, 256 + k * 128:256 + (k + 1) * 128], ones[:, :], diag[:, 4 + k, :],
                                   start=True, stop=True)
                ins.then_inc(rows_ready, 1)
                pe.wait_ge(step_ready, b + 1)
                for ch in range(2):
                    for jh in range(2):
                        t.matmul(xt_ps[:, ch:ch + 1], step[:, jh, ch * CH:(ch + 1) * CH], cols(DSM)[:, jh:jh + 1],
                                 start=(jh == 0), stop=(jh == 1))
                for jh in range(2):
                    ins = t.matmul(h_ps[:, 0:C], mrep[:, jh, :], step[:, jh, :], start=(jh == 0), stop=(jh == 1))
                ins.then_inc(mean_ready, 1)
                pe.wait_ge(gramc_ready, b + 1)
                for ih in range(2):
                    for jh in range(2):
                        ins = t.matmul(o_ps[:, ih * C:(ih + 1) * C], gramc[:, jh, ih * CH:(ih + 1) * CH], full[:, jh, :],
                                       start=(jh == 0), stop=(jh == 1))
                ins.then_inc(cov_ready, 1)

            def stats_variance(b):
                pe.wait_ge(prod_ready, b + 1)
                for ch in range(2):
                    for ih in range(2):
                        ins = t.matmul(g_ps[:, 8 + ch:9 + ch], prod[:, ih, ch * CH:(ch + 1) * CH], ones[:, 0:1],
                                       start=(ih == 0), stop=(ih == 1))
                ins.then_inc(var1_sums, 1)

            def stats_moments(b):
                pe.wait_ge(mom_ready, b + 1)
                t.matmul(g_ps[:, 16:20], group[:, :], cols(MU, 4), start=True, stop=True).then_inc(mom_group, 1)
                pe.wait_ge(diag1_ready, b + 1)
                for k in range(4):
                    ins = t.matmul(o_ps[:, k * 128:(k + 1) * 128], ones[:, :], diag[:, k, :], start=True, stop=True)
                ins.then_inc(rows1_ready, 1)

            images(pe.Fori, turn)

        @block.scalar
        def _(act):
            a = nc.scalar
            a.preload_act_table_set("natural_log_exp_and_others")
            act.sem_inc(slot_read, 2)
            act.sem_inc(xt_copied, 1)
            act.sem_inc(o_copied, 1)
            act.wait_ge(const_ready, 1)
            own = Count(act, act_done)

            def const(j):
                return cst[:, j:j + 1]

            a.activation(cols(TMP), prm[:, 3, :], ACT.Ln, bias=col[:, 63:64]).then_inc(bn_logs, 1)
            act.wait_ge(bn_logs, 1)
            a.activation(cols(GS), cols(TMP), ACT.Exp, scale=-0.5).then_inc(bn_logs, 1)

            def copy_xt(n, q):
                m = 4 * n + q
                act.wait_ge(xt_filled, m + 3)
                act.wait_ge(h_filled, m + 1)
                a.activation(xt[:, q % 2, :, :, :].rearrange("p j r w -> p (j r w)"), xt_ps[:, :], ACT.Copy
                             ).then_inc(xt_copied, 1)

            def log(unit, n, hf, which):
                s = SLOTS * unit + which
                src = slot[(hf + which) % 2]
                act.wait_ge(slot_filled, s + 1)
                if which == 0 and some(unit - 1):
                    act.wait_ge(z_ready, unit - 1)
                if which == 1 and some(unit - 1):
                    act.wait_ge(sig_used, unit - 1)
                if which == 3:
                    act.wait_ge(tail_done, unit + 1)
                if which == 4:
                    if some(32 * n):
                        act.wait_ge(pq_stored[hf], 32 * n)
                    a.activation(ut[:, hf, :], src[:, :], ACT.Copy).then_inc(slot_read, 1)
                else:
                    a.activation(logs[:, hf, which, :], src[:, :], ACT.Ln, bias=const(C_EPS)).then_inc(slot_read, 1)

            def square_contrasts(unit, hf):
                act.wait_ge(slopes, unit + 1)
                a.activation(logs[:, hf, 2, :], logs[:, hf, 2, :], ACT.Square, scale=CUBIC_SCALE).then_inc(squares, 1)
                act.wait_ge(quad_ready, unit + 1)
                a.activation(square[:, hf, :], logs[:, hf, 1, :], ACT.Square, scale=LINEAR_SCALE).then_inc(squares, 1)
                a.activation(logs[:, hf, 0, :], logs[:, hf, 0, :], ACT.Square, scale=QUAD_SCALE).then_inc(squares, 1)

            def sigmoid(unit, hf, steps):
                lk = logs[:, hf, 1, :]
                if 0 in steps:
                    a.activation(lk, lk, ACT.Exp, bias=col[:, GB + hf:GB + hf + 1], scale=col[:, GS + hf:GS + hf + 1]
                                 ).then_inc(act_done, own.one())
                if 1 in steps:
                    act.wait_ge(act_done, own.now())
                    a.activation(lk, lk, ACT.Ln, bias=const(C_ONE)).then_inc(act_done, own.one())
                if 2 in steps:
                    act.wait_ge(act_done, own.now())
                    a.activation(lk, lk, ACT.Exp, scale=-1.0).then_inc(act_done, own.one())

            def invert(unit, hf, steps):
                lk = logs[:, hf, 3, :]
                if 0 in steps:
                    act.wait_ge(z_ready, unit + 1)
                    a.activation(lk, lk, ACT.Ln, bias=const(C_TINY)).then_inc(act_done, own.one())
                if 1 in steps:
                    act.wait_ge(act_done, own.now())
                    a.activation(lk, lk, ACT.Exp, scale=0.5).then_inc(act_done, own.one())
                if 2 in steps:
                    act.wait_ge(act_done, own.now())
                    a.activation(lk, lk, ACT.Ln, bias=const(C_EPS)).then_inc(act_done, own.one())
                if 3 in steps:
                    act.wait_ge(act_done, own.now())
                    a.activation(lk, lk, ACT.Exp, scale=-1.0).then_inc(inv_ready, 1)

            def copy_out(n, unit, hf, d, k, stored):
                act.wait_ge(o_filled, 2 * unit + d + 3)
                if hf == 0 and d == 0 and some(stored):
                    act.wait_ge(o_stored[k], stored)
                a.activation(o_sb[:, k, 4 * d:4 * d + 4, hf * CH:(hf + 1) * CH],
                             o_ps[:, :].rearrange("p (r c) -> p r c", c=CH), ACT.Copy).then_inc(o_copied, 1)

            def half_chunk(s, i, k, hf, A, Bs, Cs, Ds, first):
                n = 16 * s + 2 * i + k
                nb, nC, nd = n - 16, n - 32, n - 48
                u, ud = 2 * nC + hf, 2 * nd + hf
                tail = Cs and not first
                if Cs:
                    log(u, nC, hf, 0)
                if Bs:
                    copy_xt(nb, 2 * hf)
                if tail:
                    square_contrasts(u - 1, 1 - hf)
                if Cs:
                    log(u, nC, hf, 1)
                if tail:
                    sigmoid(u - 1, 1 - hf, (0,))
                if Cs:
                    log(u, nC, hf, 2)
                if Bs:
                    copy_xt(nb, 2 * hf + 1)
                if tail:
                    sigmoid(u - 1, 1 - hf, (1,))
                if Ds:
                    copy_out(nd, ud, hf, 0, k, 16 * (8 * (s - 3) + i))
                if tail:
                    invert(u - 1, 1 - hf, (0,))
                if Cs:
                    log(u, nC, hf, 3)
                if tail:
                    invert(u - 1, 1 - hf, (1,))
                    sigmoid(u - 1, 1 - hf, (2,))
                    invert(u - 1, 1 - hf, (2,))
                if Cs:
                    log(u, nC, hf, 4)
                if tail:
                    invert(u - 1, 1 - hf, (3,))
                if Ds:
                    copy_out(nd, ud, hf, 1, k, None)

            def turn(s, A, Bs, Cs, Ds):
                def pair(i, first):
                    for k in range(2):
                        for hf in range(2):
                            half_chunk(s, i, k, hf, A, Bs, Cs, Ds, first and k == 0 and hf == 0)
                pair(0, True)
                with own.loop(1, PAIRS, ACT_PAIR if Cs else 0) as i:
                    pair(i, False)
                if Cs:
                    u = 32 * (s - 1)
                    square_contrasts(u - 1, 1)
                if A:
                    guess_root(s, var_ready, VAR, RS, rs_guess)
                if Cs:
                    sigmoid(u - 1, 1, (0, 1, 2))
                    invert(u - 1, 1, (0, 1, 2, 3))
                if A:
                    softmax_exp(s)
                if Cs:
                    act.wait_ge(gate_arg, s - 1)
                    a.activation(gate[:, 4:6], gate[:, 2:4], ACT.Exp).then_inc(gate_exp, 1)
                if A:
                    guess_root(s, var1_ready, V1, R1, rs1_guess)

            def guess_root(b, ready, var, rs, guess):
                act.wait_ge(ready, b + 1)
                a.activation(cols(rs), cols(var), ACT.Ln, bias=const(C_GN)).then_inc(act_done, own.one())
                act.wait_ge(act_done, own.now())
                a.activation(cols(rs), cols(rs), ACT.Exp, scale=-0.5).then_inc(guess, 1)

            def softmax_exp(b):
                act.wait_ge(logits_ready, b + 1)
                for h in range(2):
                    a.activation(attn[:, h, :], attn[:, h, :], ACT.Exp,
                                 bias=cols(NMAX)[:, h:h + 1], accum_out=cols(ESUM)[:, h:h + 1]).then_inc(act_done, own.one())
                act.wait_ge(act_done, own.now())
                a.activation(cols(TMP), cols(ESUM), ACT.Copy).then_inc(exp_ready, 1)

            images(lambda lo, hi: own.loop(lo, hi, ACT_IMAGE), turn)

        @block.vector
        def _(dve):
            d = nc.vector
            dve.sem_inc(tail_done, 2)
            dve.sem_inc(h_copied, 1)
            own = Count(dve, dve_done)

            def apart():
                dve.sem_inc(dve_apart, 1)

            dve.wait_ge(pool_const, POOL_CONST)
            dve.wait_ge(const_loaded, 16 * 9)
            d.memset(zeros[:, :], 0.0).then_inc(dve_done, own.one())
            d.memset(col[:, 63:64], BN_EPS).then_inc(dve_done, own.one())
            d.tensor_scalar(gate[:, 6:8], prm[:, 4, :], -1.0, None, ALU.mult).then_inc(dve_done, own.one())
            dve.wait_ge(dve_done, own.now())
            d.tensor_copy(hid[:, 1:2], hid[:, 0:1]).then_inc(const_ready, 1)
            dve.wait_ge(bn_logs, 2)
            newton_v, y = cols(V1), cols(GS)
            d.tensor_scalar(newton_v, prm[:, 3, :], BN_EPS, None, ALU.add).then_inc(dve_done, own.one())

            def newton(var, y):
                dve.wait_ge(dve_done, own.now())
                d.tensor_tensor(cols(TMP), var, y, ALU.mult).then_inc(dve_done, own.one())
                dve.wait_ge(dve_done, own.now())
                d.tensor_tensor(cols(TMP), cols(TMP), y, ALU.mult).then_inc(dve_done, own.one())
                dve.wait_ge(dve_done, own.now())
                d.tensor_scalar(cols(TMP), cols(TMP), -0.5, 1.5, ALU.mult, ALU.add).then_inc(dve_done, own.one())
                dve.wait_ge(dve_done, own.now())
                d.tensor_tensor(y, y, cols(TMP), ALU.mult).then_inc(dve_done, own.one())
                dve.wait_ge(dve_done, own.now())
            newton(newton_v, y)
            d.tensor_tensor(y, y, prm[:, 0, :], ALU.mult).then_inc(dve_done, own.one())
            dve.wait_ge(dve_done, own.now())
            d.tensor_tensor(cols(GB), y, prm[:, 2, :], ALU.mult).then_inc(dve_done, own.one())
            dve.wait_ge(dve_done, own.now())
            d.tensor_tensor(cols(GB), cols(GB), prm[:, 1, :], ALU.subtract).then_inc(dve_done, own.one())
            d.tensor_scalar(y, y, -1.0 / SLOPE, None, ALU.mult).then_inc(dve_done, own.one())
            dve.wait_ge(dve_done, own.now())

            def copy_h(n, k, q, first, stored):
                m = 4 * n + q
                dve.wait_ge(h_filled, m + 3)
                if q == 0 and some(stored):
                    dve.wait_ge(h_stored[k], stored)
                apart()
                d.tensor_tensor_reduce(h_out[:, k, 2 * q:2 * q + 2, :].rearrange("p r c -> p (r c)"), h_ps[:, :],
                                       shift[:, :, :].rearrange("p r c -> p (r c)"), 1.0,
                                       mx[:, (q - 1) % 4:(q - 1) % 4 + 1], ALU.add, ALU.max,
                                       mx[:, q:q + 1]).then_inc(h_copied, 1)
                dve.wait_ge(h_copied, m + 2)

            def min_h(i, k, hf):
                at = 4 * i + 2 * k + hf
                d.tensor_reduce(mins[:, at:at + 1] if isinstance(at, int) else mins[:, bass.ds(at, 1)],
                                h_out[:, k, 4 * hf:4 * hf + 4, :].rearrange("p r c -> p (r c)"), AX_X, ALU.min
                                ).then_inc(dve_done, own.one())

            def p_plus_q(n, unit, hf):
                dve.wait_ge(pq_loaded[hf], 32 * (n + 1))
                d.scalar_tensor_tensor(pd[:, hf, :], qd[:, hf, :], cols(NE)[:, hf:hf + 1], pd[:, hf, :],
                                       ALU.mult, ALU.add).then_inc(sum_ready, 1)

            def mid_contrast(unit, hf):
                dve.wait_ge(slot_read, 2 + SLOTS * unit + 3)
                dve.wait_ge(low_ready, unit + 1)
                d.tensor_tensor(logs[:, hf, 1, :], logs[:, hf, 1, :], logs[:, hf, 2, :], ALU.subtract).then_inc(dve_done, own.one())

            def high_contrast(unit, hf):
                dve.wait_ge(slot_read, 2 + SLOTS * unit + 4)
                d.tensor_tensor(logs[:, hf, 3, :], logs[:, hf, 2, :], logs[:, hf, 3, :], ALU.subtract).then_inc(high_ready, 1)

            def cubic_and_slope(unit, hf):
                L = [logs[:, hf, k, :] for k in range(4)]
                dve.wait_ge(high_ready, unit + 1)
                d.tensor_tensor(L[2], square[:, hf, :], L[3], ALU.add).then_inc(dve_done, own.one())
                dve.wait_ge(dve_done, own.now())
                d.scalar_tensor_tensor(L[2], L[1], 2.0, L[2], ALU.mult, ALU.subtract).then_inc(dve_done, own.one())
                dve.wait_ge(dve_done, own.now())
                d.scalar_tensor_tensor(L[1], L[2], -0.3, L[1], ALU.mult, ALU.add, accum_out=col[:, TACC:TACC + 1]
                                       ).then_inc(slopes, 1)

            def add_slopes(unit, hf):
                dve.wait_ge(slopes, unit + 1)
                d.tensor_tensor(cols(ACC)[:, hf:hf + 1], cols(ACC)[:, hf:hf + 1], col[:, TACC:TACC + 1], ALU.add).then_inc(dve_done, own.one())

            def norms(unit, hf):
                z = logs[:, hf, 3, :]
                dve.wait_ge(squares, 3 * unit + 2)
                d.tensor_tensor(z, square[:, hf, :], logs[:, hf, 2, :], ALU.add).then_inc(dve_done, own.one())
                dve.wait_ge(squares, 3 * unit + 3)
                dve.wait_ge(dve_done, own.now())
                d.tensor_tensor(z, z, logs[:, hf, 0, :], ALU.add).then_inc(dve_done, own.one())
                dve.wait_ge(dve_done, own.now())
                d.tensor_tensor(z, z, square[:, hf, :], ALU.mult).then_inc(z_ready, 1)

            def finish(unit, hf):
                sim, sig, prod = square[:, hf, :], logs[:, hf, 1, :], logs[:, hf, 3, :]
                dve.wait_ge(inv_ready, unit + 1)
                d.tensor_tensor(sim, sim, logs[:, hf, 3, :], ALU.mult).then_inc(dve_done, own.one())
                dve.wait_ge(dve_done, own.now())
                d.tensor_tensor(prod, sig, sim, ALU.mult).then_inc(sig_used, 1)
                dve.wait_ge(x1_ready, unit + 1)
                d.scalar_tensor_tensor(ut[:, hf, :], sim, -1.0, ut[:, hf, :], ALU.add, ALU.mult).then_inc(dve_done, own.one())
                dve.wait_ge(sig_used, unit + 1)
                d.tensor_tensor(x1t[:, hf, :], x1t[:, hf, :], prod, ALU.add).then_inc(tail_done, 1)

            def half_chunk(s, i, k, hf, A, Bs, Cs, Ds, first):
                n = 16 * s + 2 * i + k
                nb, nC, nd = n - 16, n - 32, n - 48
                u = 2 * nC + hf
                tail = Cs and not first
                if Ds:
                    p_plus_q(nd, 2 * nd + hf, hf)
                if tail:
                    norms(u - 1, 1 - hf)
                if Bs:
                    copy_h(nb, k, 2 * hf, first, 16 * (8 * (s - 1) + i))
                if Cs:
                    mid_contrast(u, hf)
                    high_contrast(u, hf)
                if Bs:
                    copy_h(nb, k, 2 * hf + 1, first, None)
                if Cs:
                    cubic_and_slope(u, hf)
                if Bs:
                    min_h(i, k, hf)
                if tail:
                    finish(u - 1, 1 - hf)
                if Cs:
                    add_slopes(u, hf)

            def turn(s, A, Bs, Cs, Ds):
                if Bs:
                    d.memset(mx[:, :], -HUGE).then_inc(dve_done, own.one())
                if Cs:
                    d.memset(cols(ACC), 0.0).then_inc(dve_done, own.one())
                dve.wait_ge(dve_done, own.now())

                def pair(i, first):
                    for k in range(2):
                        for hf in range(2):
                            half_chunk(s, i, k, hf, A, Bs, Cs, Ds, first and k == 0 and hf == 0)
                pair(0, True)
                with own.loop(1, PAIRS, (DVE_MIN_PAIR if Bs else 0) + (DVE_PAIR if Cs else 0)) as i:
                    pair(i, False)
                dve.wait_ge(dve_done, own.now())
                u = 32 * (s - 1)
                if Bs:
                    value_range(s - 1)
                if A:
                    stats_variance(s, Bs)
                    stats_columns(s)
                if Cs:
                    norms(u - 1, 1)
                if A:
                    stats_logits(s)
                    stats_step(s, Bs)
                if Cs:
                    finish(u - 1, 1)
                if A:
                    stats_mean(s)
                if Cs:
                    excite_sums(s - 2)
                if A:
                    stats_product(s)
                if Cs:
                    excite_hidden(s - 2)
                if A:
                    stats_moments(s)
                if Cs:
                    excite_gate(s - 2)
                if A:
                    stats_root(s)
                if Cs:
                    excite_done(s - 2)
                if A:
                    stats_mix(s)

            def value_range(b):
                d.tensor_copy(rr[:, 0:1], mx[:, 3:4]).then_inc(dve_done, own.one())
                d.tensor_reduce(col[:, MNP:MNP + 1], mins[:, :], AX_X, ALU.min).then_inc(dve_done, own.one())
                dve.wait_ge(dve_done, own.now())
                d.tensor_scalar(rr[:, 1:2], col[:, MNP:MNP + 1], -1.0, None, ALU.mult).then_inc(dve_done, own.one())
                dve.wait_ge(dve_done, own.now())
                d.tensor_copy(mx[:, 0:1], rr[:, 0:1]).then_inc(range_in, 1)
                dve.wait_ge(range_out, b + 1)
                d.scalar_tensor_tensor(col[:, RNG:RNG + 1], rr[:, 2:3], rr[:, 3:4], cst[:, 0:1], ALU.add, ALU.add).then_inc(dve_done, own.one())
                d.tensor_copy(col[:, NEGMIN:NEGMIN + 1], rr[:, 3:4]).then_inc(dve_done, own.one())
                dve.wait_ge(dve_done, own.now())
                d.reciprocal(col[:, INV:INV + 1], col[:, RNG:RNG + 1]).then_inc(dve_done, own.one())
                d.tensor_scalar(cols(XS), cols(RI), col[:, RNG:RNG + 1], None, ALU.mult).then_inc(dve_done, own.one())
                d.tensor_scalar(cols(XK), cols(RI), col[:, NEGMIN:NEGMIN + 1], -1.0, ALU.mult, ALU.mult).then_inc(dve_done, own.one())
                dve.wait_ge(dve_done, own.now())
                d.tensor_tensor(cols(XK), cols(XK), cols(M1), ALU.add).then_inc(dve_done, own.one())
                dve.wait_ge(dve_done, own.now())
                d.tensor_copy(mx[:, 1:2], rr[:, 0:1]).then_inc(range_ready, 1)

            def excite_sums(b):
                dve.wait_ge(dve_done, own.now())
                d.tensor_scalar(gate[:, 0:2], cols(ACC), 1.0 / (SLOPE * PIX), None, ALU.mult).then_inc(sums_ready, 1)

            def excite_hidden(b):
                dve.wait_ge(hidden_ps, b + 1)
                d.tensor_scalar(hid[:, 2:3], xt_ps[0:HIDDEN, 256:257], hid[:, 1:2], 0.0, ALU.add, ALU.max
                                ).then_inc(hidden_ready, 1)

            def excite_gate(b):
                dve.wait_ge(gate_ps, b + 1)
                d.scalar_tensor_tensor(gate[:, 2:4], xt_ps[:, 264:266], -1.0, gate[:, 6:8], ALU.mult, ALU.add).then_inc(dve_done, own.one())
                dve.wait_ge(dve_done, own.now())
                d.tensor_scalar(gate[:, 2:4], gate[:, 2:4], EXP_MAX, None, ALU.min).then_inc(gate_arg, 1)

            def excite_done(b):
                dve.wait_ge(gate_exp, b + 1)
                d.tensor_scalar(gate[:, 4:6], gate[:, 4:6], 1.0, None, ALU.add).then_inc(dve_done, own.one())
                dve.wait_ge(dve_done, own.now())
                d.reciprocal(cols(NE), gate[:, 4:6]).then_inc(dve_done, own.one())
                dve.wait_ge(dve_done, own.now())
                d.tensor_scalar(cols(NE), cols(NE), -1.0, None, ALU.mult).then_inc(dve_done, own.one())
                dve.wait_ge(dve_done, own.now())

            def rows_of(vectors):
                for k, vec in enumerate(vectors):
                    for h in range(2):
                        d.tensor_scalar(diag[:, 2 * k + h, :], ident[:, :], vec[:, h:h + 1], None, ALU.mult).then_inc(dve_done, own.one())

            def stats_variance(b, stored):
                if stored:
                    dve.wait_ge(h_stored[0], 16 * PAIRS * b)
                dve.wait_ge(xa_used, 2 + 2 * CHUNKS * (b + 1))
                d.tensor_copy(gram[:, 0, :], g_ps[:, 0:C]).then_inc(dve_done, own.one())
                d.tensor_copy(gram[:, 1, CH:C], g_ps[:, C + 1:C + 1 + CH]).then_inc(dve_done, own.one())
                d.tensor_copy(col[:, SUM:SUM + 1], g_ps[:, C:C + 1]).then_inc(dve_done, own.one())
                dve.wait_ge(dve_done, own.now())
                d.tensor_copy(col[:, SUM + 1:SUM + 2], g_ps[:, C + 1 + CH:C + 2 + CH]).then_inc(gram_copied, 1)
                dve.wait_ge(gram_turned, b + 1)
                d.tensor_copy(gram[:, 1, 0:CH], xt_ps[:, 0:CH]).then_inc(dve_done, own.one())
                for h in range(2):
                    apart()
                    d.tensor_tensor_reduce(junk, gram[:, h, h * CH:(h + 1) * CH], ident[:, :], 1.0, 0.0,
                                           ALU.mult, ALU.add, col[:, SQ + h:SQ + h + 1]).then_inc(dve_done, own.one())
                    dve.wait_ge(dve_done, own.now())
                d.tensor_copy(junk[:, 0:1], col[:, SQ:SQ + 1]).then_inc(gram_whole, 1)
                dve.wait_ge(group_sums, b + 1)
                d.tensor_scalar(cols(MEAN, 4), h_ps[:, 0:4], 1.0 / PIX, None, ALU.mult).then_inc(dve_done, own.one())
                dve.wait_ge(dve_done, own.now())
                d.tensor_tensor(cols(TMP), cols(MEAN), cols(MEAN), ALU.mult).then_inc(dve_done, own.one())
                dve.wait_ge(dve_done, own.now())
                d.tensor_tensor(cols(VAR), cols(VAR), cols(TMP), ALU.subtract).then_inc(var_ready, 1)

            def stats_columns(b):
                dve.wait_ge(rs_guess, b + 1)
                d.tensor_scalar(cols(VAR), cols(VAR), GN_EPS, None, ALU.add).then_inc(dve_done, own.one())
                newton(cols(VAR), cols(RS))
                d.tensor_scalar(cols(NMEAN), cols(MEAN), -1.0, None, ALU.mult).then_inc(dve_done, own.one())
                d.scalar_tensor_tensor(cols(WGT), cols(MEAN), float(PIX), cols(SUM), ALU.mult, ALU.subtract).then_inc(dve_done, own.one())
                d.tensor_scalar(cols(GR), cols(RS), col[:, GAM:GAM + 1], None, ALU.mult).then_inc(dve_done, own.one())
                d.scalar_tensor_tensor(cols(DSM), cols(SUM), 1.0 / PIX, cols(MEAN), ALU.mult, ALU.subtract).then_inc(dve_done, own.one())
                d.tensor_scalar(cols(NSP), cols(SUM), -1.0 / PIX, None, ALU.mult).then_inc(dve_done, own.one())
                rows_of((cols(SUM), cols(MEAN), cols(RS)))
                dve.wait_ge(dve_done, own.now())
                d.tensor_scalar(mrep[:, 0, :], ones[:, :], cols(NMEAN)[:, 0:1], None, ALU.mult).then_inc(diag_ready, 1)
                d.tensor_scalar(mrep[:, 1, :], ones[:, :], cols(NMEAN)[:, 1:2], None, ALU.mult).then_inc(dve_done, own.one())

            def stats_logits(b):
                dve.wait_ge(rows_ready, b + 1)
                d.tensor_copy(rows[:, 0:2, :].rearrange("p k c -> p (k c)"), xt_ps[:, :]).then_inc(dve_done, own.one())
                d.tensor_copy(rows[:, 2, :], h_ps[:, 256:512]).then_inc(dve_done, own.one())
                dve.wait_ge(dve_done, own.now())
                for h in range(2):
                    d.scalar_tensor_tensor(attn[:, h, :], rows[:, 0, :], cols(NMEAN)[:, h:h + 1], gram[:, h, :],
                                           ALU.mult, ALU.add).then_inc(dve_done, own.one())
                dve.wait_ge(dve_done, own.now())
                for h in range(2):
                    d.scalar_tensor_tensor(attn[:, h, :], rows[:, 1, :], cols(WGT)[:, h:h + 1], attn[:, h, :],
                                           ALU.mult, ALU.add).then_inc(dve_done, own.one())
                dve.wait_ge(dve_done, own.now())
                for h in range(2):
                    d.scalar_tensor_tensor(attn[:, h, :], attn[:, h, :], cols(RS)[:, h:h + 1], rows[:, 2, :],
                                           ALU.mult, ALU.mult).then_inc(dve_done, own.one())
                dve.wait_ge(dve_done, own.now())
                for h in range(2):
                    d.tensor_reduce(cols(NMAX)[:, h:h + 1], attn[:, h, :], AX_X, ALU.max).then_inc(dve_done, own.one())
                dve.wait_ge(dve_done, own.now())
                d.tensor_scalar(cols(NMAX), cols(NMAX), -1.0, None, ALU.mult).then_inc(logits_ready, 1)

            def stats_step(b, stored):
                if stored:
                    dve.wait_ge(h_stored[1], 16 * PAIRS * b)
                dve.wait_ge(exp_ready, b + 1)
                d.reciprocal(cols(ESUM), cols(ESUM)).then_inc(dve_done, own.one())
                dve.wait_ge(dve_done, own.now())
                d.tensor_tensor(cols(GR), cols(GR), cols(ESUM), ALU.mult).then_inc(dve_done, own.one())
                dve.wait_ge(dve_done, own.now())
                for h in range(2):
                    d.tensor_scalar(step[:, h, :], attn[:, h, :], cols(GR)[:, h:h + 1], None, ALU.mult).then_inc(dve_done, own.one())
                dve.wait_ge(dve_done, own.now())
                for h in range(2):
                    at = step[:, h, h * CH:(h + 1) * CH]
                    d.tensor_tensor(at, at, diag[:, 4 + h, :], ALU.add).then_inc(dve_done, own.one())
                dve.wait_ge(dve_done, own.now())
                for h in range(2):
                    d.tensor_copy(full[:, h, :], step[:, h, :]).then_inc(dve_done, own.one())
                dve.wait_ge(dve_done, own.now())
                for h in range(2):
                    at = full[:, h, h * CH:(h + 1) * CH]
                    d.tensor_tensor(at, at, ident[:, :], ALU.add).then_inc(dve_done, own.one())
                dve.wait_ge(dve_done, own.now())
                d.tensor_copy(junk[:, 0:1], col[:, SQ:SQ + 1]).then_inc(step_ready, 1)
                d.scalar_tensor_tensor(gramc[:, 0, :], rows[:, 0, :], cols(NSP)[:, 0:1], gram[:, 0, :], ALU.mult, ALU.add).then_inc(dve_done, own.one())
                dve.wait_ge(dve_done, own.now())
                d.scalar_tensor_tensor(gramc[:, 1, :], rows[:, 0, :], cols(NSP)[:, 1:2], gram[:, 1, :], ALU.mult, ALU.add
                                       ).then_inc(gramc_ready, 1)

            def stats_mean(b):
                dve.wait_ge(mean_ready, b + 1)
                d.tensor_tensor(cols(MU), xt_ps[:, 0:2], cols(NSP), ALU.subtract).then_inc(dve_done, own.one())
                dve.wait_ge(dve_done, own.now())
                d.tensor_tensor(cols(M2), cols(MU), cols(MU), ALU.mult).then_inc(dve_done, own.one())
                dve.wait_ge(dve_done, own.now())

            def stats_product(b):
                dve.wait_ge(cov_ready, b + 1)
                d.tensor_tensor(prod[:, 0, :], full[:, 0, :], o_ps[:, 0:C], ALU.mult).then_inc(dve_done, own.one())
                dve.wait_ge(dve_done, own.now())
                d.tensor_tensor(prod[:, 1, :], full[:, 1, :], o_ps[:, C:2 * C], ALU.mult).then_inc(prod_ready, 1)

            def stats_moments(b):
                dve.wait_ge(var1_sums, b + 1)
                d.scalar_tensor_tensor(cols(M2), g_ps[:, 8:10], 1.0 / PIX, cols(M2), ALU.mult, ALU.add).then_inc(mom_ready, 1)

            def stats_root(b):
                dve.wait_ge(mom_group, b + 1)
                d.tensor_copy(cols(M1, 4), g_ps[:, 16:20]).then_inc(dve_done, own.one())
                dve.wait_ge(dve_done, own.now())
                d.tensor_tensor(cols(TMP), cols(M1), cols(M1), ALU.mult).then_inc(dve_done, own.one())
                dve.wait_ge(dve_done, own.now())
                d.tensor_tensor(cols(V1), cols(V1), cols(TMP), ALU.subtract).then_inc(var1_ready, 1)
                dve.wait_ge(rs1_guess, b + 1)
                d.tensor_scalar(cols(V1), cols(V1), GN_EPS, None, ALU.add).then_inc(dve_done, own.one())
                newton(cols(V1), cols(R1))
                d.tensor_tensor(cols(RI), cols(V1), cols(R1), ALU.mult).then_inc(dve_done, own.one())
                rows_of((cols(R1), cols(M1)))
                dve.wait_ge(dve_done, own.now())
                d.tensor_copy(junk[:, 0:1], col[:, SQ:SQ + 1]).then_inc(diag1_ready, 1)

            def stats_mix(b):
                dve.wait_ge(rows1_ready, b + 1)
                d.tensor_copy(rows[:, 0:2, :].rearrange("p k c -> p (k c)"), o_ps[:, :]).then_inc(dve_done, own.one())
                d.tensor_copy(rows[:, 2, :], h_ps[:, 0:C]).then_inc(dve_done, own.one())
                dve.wait_ge(dve_done, own.now())
                for h in range(2):
                    d.tensor_tensor(mix[:, h, :], full[:, h, :], rows[:, 0, :], ALU.mult).then_inc(dve_done, own.one())
                d.tensor_tensor(rows[:, 2, :], rows[:, 2, :], rows[:, 1, :], ALU.subtract).then_inc(dve_done, own.one())
                dve.wait_ge(dve_done, own.now())
                d.tensor_tensor(shift[:, 0, :], rows[:, 2, :], rows[:, 0, :], ALU.mult).then_inc(dve_done, own.one())
                dve.wait_ge(dve_done, own.now())
                d.tensor_copy(shift[:, 1, :], shift[:, 0, :]).then_inc(mix_ready, 1)

            images(lambda lo, hi: own.loop(lo, hi, DVE_IMAGE), turn)


_INS = ['x', 'L0_conv_gamma', 'L1_conv_w1', 'L1_conv_b1', 'L1_conv_w2', 'L1_conv_b2', 'L1_conv_gamma',
        'L1_conv_beta', 'L1_conv_moving_mean', 'L1_conv_moving_var']
_OUTS = [((B, H, W, C), 'float32')]


def kernel(**inputs):
    import numpy as _np
    import concourse.bacc as _bacc
    from concourse import mybir as _mybir
    from concourse.bass_utils import run_bass_kernel_spmd as _run

    nc = _bacc.Bacc("TRN2", target_bir_lowering=False, num_devices=1)
    arrays, args = {}, []
    for name in _INS:
        a = _np.ascontiguousarray(inputs[name])
        arrays[f"in_{name}_dram"] = a
        args.append(nc.dram_tensor(f"in_{name}_dram", a.shape, _mybir.dt.from_np(a.dtype), kind="ExternalInput").ap())
    for i, (shape, dtype) in enumerate(_OUTS):
        dt = _mybir.dt.from_np(_np.dtype(dtype))
        args.append(nc.dram_tensor(f"out_{i}_dram", shape, dt, kind="ExternalOutput").ap())
    mk_conv_preact(nc, *args)
    r = _run(nc, [arrays], core_ids=[0])
    got = tuple(r.results[0][f"out_{i}_dram"] for i in range(len(_OUTS)))
    return got[0]
```
